# Optimizing a Trainium2 kernel written in Bass

```python
import numpy as np
import jax
import jax.numpy as jnp

def _softmax(x, axis=-1):
    return jax.nn.softmax(x, axis=axis)
def _gelu(x):
    return jax.nn.gelu(x, approximate=True)
def _silu(x):
    return jax.nn.silu(x)
def _sigmoid(x):
    return jax.nn.sigmoid(x)
def _layernorm(x, axis=-1, eps=1e-5):
    m = jnp.mean(x, axis=axis, keepdims=True)
    v = jnp.var(x, axis=axis, keepdims=True)
    return (x - m) / jnp.sqrt(v + eps)
def _scatter_add(tgt, idx, src, axis=0):
    return tgt.at[idx].add(src)
def _segment_sum(src, seg, n):
    return jax.ops.segment_sum(src, seg, n)

kernel_name = 'mk_adj_seq_d1_adj_512_59c920'

def setup_inputs(seed: int = 0):
    np.random.seed(seed)
    _w = jnp.asarray
    def _rec_inputs():
        import jax
        import jax.numpy as jnp
        _gk = jax.random.key(seed)
        x = -0.0005207 + 1.001 * jax.random.normal(jax.random.fold_in(_gk, 1), (128, 64, 512), jnp.float32)
        _a = jax.random.bernoulli(jax.random.fold_in(_gk, 2), 0.0625, (128, 64, 64))
        _a = jnp.logical_or(_a, jnp.swapaxes(_a, -1, -2))
        _a = jnp.logical_or(_a, jnp.eye(64, dtype=bool))
        adj = _a
        return x, adj
    x, adj = _rec_inputs()
    def _L0_gnn_setup():
        import jax, jax.numpy as jnp
        import numpy as np
        HIDDEN = 512
        HEADS = 8
        HEAD_DIM = HIDDEN // HEADS
        D_FF = 4 * HIDDEN
        NEG = -1000000000.0

        def _layernorm(x, g, b, eps=1e-05):
            mu = jnp.mean(x, axis=-1, keepdims=True)
            var = jnp.var(x, axis=-1, keepdims=True)
            return (x - mu) * jax.lax.rsqrt(var + eps) * g + b
        key = jax.random.key(seed)
        ks = jax.random.split(key, 16)
        B, S = (2, 2048)
        s = 1.0 / np.sqrt(HIDDEN)
        inp = {'x': jax.random.normal(ks[0], (B, S, HIDDEN), dtype=jnp.float32), 'adj_mask': jax.random.bernoulli(ks[1], 0.5, (B, S, S)), 'ln1_g': jnp.ones((HIDDEN,), jnp.float32), 'ln1_b': jnp.zeros((HIDDEN,), jnp.float32), 'ln2_g': jnp.ones((HIDDEN,), jnp.float32), 'ln2_b': jnp.zeros((HIDDEN,), jnp.float32), 'Wq': jax.random.uniform(ks[2], (HIDDEN, HIDDEN), jnp.float32, -s, s), 'bq': jnp.zeros((HIDDEN,), jnp.float32), 'Wk': jax.random.uniform(ks[3], (HIDDEN, HIDDEN), jnp.float32, -s, s), 'bk': jnp.zeros((HIDDEN,), jnp.float32), 'Wv': jax.random.uniform(ks[4], (HIDDEN, HIDDEN), jnp.float32, -s, s), 'bv': jnp.zeros((HIDDEN,), jnp.float32), 'Wo': jax.random.uniform(ks[5], (HIDDEN, HIDDEN), jnp.float32, -s, s), 'bo': jnp.zeros((HIDDEN,), jnp.float32), 'W1': jax.random.uniform(ks[6], (HIDDEN, D_FF), jnp.float32, -s, s), 'b1': jnp.zeros((D_FF,), jnp.float32), 'W2': jax.random.uniform(ks[7], (D_FF, HIDDEN), jnp.float32, -1.0 / np.sqrt(D_FF), 1.0 / np.sqrt(D_FF)), 'b2': jnp.zeros((HIDDEN,), jnp.float32)}
        return inp
    _L0_gnn_all = _L0_gnn_setup()
    _L0_gnn_in = {k: v for k, v in _L0_gnn_all.items() if k in ('ln1_g', 'ln1_b', 'ln2_g', 'ln2_b', 'Wq', 'bq', 'Wk', 'bk', 'Wv', 'bv', 'Wo', 'bo', 'W1', 'b1', 'W2', 'b2', )}
    del _L0_gnn_all

    return {
        "x": x,
        "adj": adj,
        "L0_gnn_ln1_g": _L0_gnn_in["ln1_g"],
        "L0_gnn_ln1_b": _L0_gnn_in["ln1_b"],
        "L0_gnn_ln2_g": _L0_gnn_in["ln2_g"],
        "L0_gnn_ln2_b": _L0_gnn_in["ln2_b"],
        "L0_gnn_Wq": _L0_gnn_in["Wq"],
        "L0_gnn_bq": _L0_gnn_in["bq"],
        "L0_gnn_Wk": _L0_gnn_in["Wk"],
        "L0_gnn_bk": _L0_gnn_in["bk"],
        "L0_gnn_Wv": _L0_gnn_in["Wv"],
        "L0_gnn_bv": _L0_gnn_in["bv"],
        "L0_gnn_Wo": _L0_gnn_in["Wo"],
        "L0_gnn_bo": _L0_gnn_in["bo"],
        "L0_gnn_W1": _L0_gnn_in["W1"],
        "L0_gnn_b1": _L0_gnn_in["b1"],
        "L0_gnn_W2": _L0_gnn_in["W2"],
        "L0_gnn_b2": _L0_gnn_in["b2"],
    }

def reference(x, adj, L0_gnn_ln1_g, L0_gnn_ln1_b, L0_gnn_ln2_g, L0_gnn_ln2_b, L0_gnn_Wq, L0_gnn_bq, L0_gnn_Wk, L0_gnn_bk, L0_gnn_Wv, L0_gnn_bv, L0_gnn_Wo, L0_gnn_bo, L0_gnn_W1, L0_gnn_b1, L0_gnn_W2, L0_gnn_b2):
    import jax
    import jax.numpy as jnp
    def _L0_gnn_ref(x, adj_mask, ln1_g, ln1_b, ln2_g, ln2_b, Wq, bq, Wk, bk, Wv, bv, Wo, bo, W1, b1, W2, b2):
        import jax, jax.numpy as jnp
        import numpy as np
        HIDDEN = 512
        HEADS = 8
        HEAD_DIM = HIDDEN // HEADS
        D_FF = 4 * HIDDEN
        NEG = -1000000000.0

        def _layernorm(x, g, b, eps=1e-05):
            mu = jnp.mean(x, axis=-1, keepdims=True)
            var = jnp.var(x, axis=-1, keepdims=True)
            return (x - mu) * jax.lax.rsqrt(var + eps) * g + b
        B, S, H = x.shape
        nx = _layernorm(x, ln1_g, ln1_b)
        q = (nx @ Wq + bq).reshape(B, S, HEADS, HEAD_DIM)
        k = (nx @ Wk + bk).reshape(B, S, HEADS, HEAD_DIM)
        v = (nx @ Wv + bv).reshape(B, S, HEADS, HEAD_DIM)
        scores = jnp.einsum('bqhd,bkhd->bhqk', q, k) / np.sqrt(HEAD_DIM)
        scores = jnp.where(adj_mask[:, None, :, :], scores, NEG)
        attn = jax.nn.softmax(scores, axis=-1)
        out = jnp.einsum('bhqk,bkhd->bqhd', attn, v).reshape(B, S, H)
        out = out @ Wo + bo
        x = x + out
        nx = _layernorm(x, ln2_g, ln2_b)
        mlp = jax.nn.gelu(nx @ W1 + b1, approximate=False) @ W2 + b2
        return x + mlp

    x = _L0_gnn_ref(x, adj, L0_gnn_ln1_g, L0_gnn_ln1_b, L0_gnn_ln2_g, L0_gnn_ln2_b, L0_gnn_Wq, L0_gnn_bq, L0_gnn_Wk, L0_gnn_bk, L0_gnn_Wv, L0_gnn_bv, L0_gnn_Wo, L0_gnn_bo, L0_gnn_W1, L0_gnn_b1, L0_gnn_W2, L0_gnn_b2)
    return x


_drawn_inputs = setup_inputs


def setup_inputs(seed=0):
    import zlib

    import numpy as np

    out = dict(_drawn_inputs(seed))
    spreads = {'L0_gnn_ln1_g': (1.0, 0.592),
     'L0_gnn_ln1_b': (0.0, 0.1),
     'L0_gnn_ln2_g': (1.0, 0.2),
     'L0_gnn_ln2_b': (0.0, 0.403),
     'L0_gnn_bq': (0.0, 0.8),
     'L0_gnn_bk': (0.0, 0.8),
     'L0_gnn_bv': (0.0, 0.1),
     'L0_gnn_bo': (0.0, 0.1),
     'L0_gnn_b1': (0.0, 0.1),
     'L0_gnn_b2': (0.0, 0.1)}
    factors = {}
    for name, (base, spread) in spreads.items():
        noise = np.random.default_rng([zlib.crc32(name.encode()), seed]).standard_normal(out[name].shape)
        drawn = base * np.exp(spread * noise) if base else spread * noise
        out[name] = jnp.asarray(drawn.astype(out[name].dtype))
    for name, factor in factors.items():
        out[name] = (out[name] * factor).astype(out[name].dtype)
    return out
```

```python
import concourse.bass as bass
from concourse import mybir
from contextlib import ExitStack


def graph_layer(nc: bass.Bass, x, adj, ln1_g, ln1_b, ln2_g, ln2_b, Wq, bq, Wk, bk, Wv, bv, Wo, bo, W1, b1, W2, b2,
                out):
    fp32 = mybir.dt.float32
    f32r = mybir.dt.float32r
    u8 = mybir.dt.uint8
    ALU = mybir.AluOpType
    ACT = mybir.ActivationFunctionType
    AX = mybir.AxisListType

    GRAPHS, NODES, DIM = x.shape
    FF = W1.shape[1]
    HEADS, DH = 8, DIM // 8
    P = 128
    EPS = 1e-5
    NEG = -1.0e9
    KEEP = 3.0e38
    QSCALE = float(DH) ** -0.5

    KC = DIM // P
    HP = HEADS // 2
    FC = FF // P
    GS = P // NODES
    SL = 4
    TOK = SL * P
    GT = TOK // NODES
    TILES = GRAPHS * NODES // TOK
    UNITS = 3 * KC
    Q0, K0, V0 = 0, KC, 2 * KC
    assert UNITS == 3 * SL and TILES % 2 == 0 and TILES >= 6 and HP == KC and GS == 2

    x_v = x.rearrange("a s d -> (a s) d").rearrange("(n t p) d -> n t p d", t=SL, p=P)
    out_v = out.rearrange("a s d -> (a s) d").rearrange("(n t p) d -> n t p d", t=SL, p=P)
    x1_v = nc.dram_tensor("x1_rows", (GRAPHS * NODES, DIM), fp32, kind="Internal").ap()\
        .rearrange("(n t p) d -> n t p d", t=SL, p=P)
    adj_v = adj.rearrange("(n g) q k -> n q g k", g=GT)

    def chunked(w):
        return w.rearrange("(c p) n -> p c n", p=P)

    def row(v):
        return v.rearrange("(a n) -> a n", a=1).to_broadcast([P, v.shape[0]])

    ctx = ExitStack()
    with ctx:
        def keep(name, shape, dt=fp32):
            return ctx.enter_context(nc.sbuf_tensor(name, shape, dt))

        def sem(name):
            return ctx.enter_context(nc.semaphore(name))

        ident = keep("ident", [P, P])
        g1_col = keep("g1_col", [P, KC])
        b1n_col = keep("b1n_col", [P, KC])
        g2_col = keep("g2_col", [P, KC])
        b2n_col = keep("b2n_col", [P, KC])
        bq_col = keep("bq_col", [P, KC])
        bk_col = keep("bk_col", [P, KC])
        bv_col = keep("bv_col", [P, KC])
        bh_col = keep("bh_col", [P, FC])
        bo_row = keep("bo_row", [P, DIM])
        by_row = keep("by_row", [P, DIM])
        neg_half = keep("neg_half", [P, 1])
        eps = keep("eps", [P, 1])
        stats = keep("stats", [P, 2, 6])
        moments = keep("moments", [P, 2, 2])
        var_eps = keep("var_eps", [P, 2, 1])
        rstd = keep("rstd", [P, 2, 1])
        rowmax = keep("rowmax", [P, GS * HP])
        rowsum = keep("rowsum", [P, GS * HP])
        rowrec = keep("rowrec", [P, GS * HP])

        CH = 4 * DIM
        ARENA = 98 * CH
        arena = ctx.enter_context(nc.sbuf_tensor("arena", [P, ARENA // 4], fp32))
        base = nc.sbuf_base - ARENA

        def at(name, slot, shape, dt=fp32):
            return nc.alloc_sbuf_tensor_at(name, shape, dt, offset=base + int(slot * CH))

        wq_hi = at("wq_hi", 0, [P, KC, DIM], f32r)
        wq_lo = at("wq_lo", 4, [P, KC, DIM], f32r)
        wk_hi = at("wk_hi", 8, [P, KC, DIM], f32r)
        wk_lo = at("wk_lo", 12, [P, KC, DIM], f32r)
        wv_hi = at("wv_hi", 16, [P, KC, DIM], f32r)
        wv_lo = at("wv_lo", 20, [P, KC, DIM], f32r)
        zT_hi = [at(f"zT_hi{j}", 32 - 8 * j, [P, KC, TOK], f32r) for j in range(2)]
        zT_lo = [at(f"zT_lo{j}", 36 - 8 * j, [P, KC, TOK], f32r) for j in range(2)]
        wo_hi = at("wo_hi", 40, [P, KC, DIM], f32r)
        wo_lo = at("wo_lo", 44, [P, KC, DIM], f32r)
        q_bd = [at(f"q_bd{j}", 64 - 16 * j, [P, HP, GT, 2, NODES]) for j in range(2)]
        kT = [at(f"kT{j}", 72 - 16 * j, [P, HP, TOK]) for j in range(2)]
        v = [at(f"v{j}", 76 - 16 * j, [P, SL, DIM]) for j in range(2)]
        xs = at("xs", 80, [P, SL, DIM])
        z = at("z", 84, [P, 2, DIM])
        xr = at("xr", 86, [P, SL, DIM])
        probs = at("probs", 90, [P, HP, GS, NODES])
        probsT = at("probsT", 91, [P, HP, P])
        oT_hi = at("oT_hi", 92, [P, HP, P], f32r)
        oT_lo = at("oT_lo", 93, [P, HP, P], f32r)
        mask = at("mask", 94, [P, 2, GT, NODES])
        adj_b = at("adj_b", 96, [P, 2, GT, NODES], u8)
        raw = [at("raw_q", 48, [P, KC, DIM]), at("raw_k", 52, [P, KC, DIM]), at("raw_v", 56, [P, KC, DIM]),
               at("raw_o", 60, [P, KC, DIM])]
        bv_rep = at("bv_rep", 90, [P, KC, P])
        w1_hi = at("w1_hi", 0, [P, KC, FF], f32r)
        w1_lo = at("w1_lo", 16, [P, KC, FF], f32r)
        raw1 = at("raw1", 32, [P, 2, FF])
        w2_hi = at("w2_hi", 32, [P, FC, DIM], f32r)
        w2_lo = at("w2_lo", 48, [P, FC, DIM], f32r)
        yT_hi = [at(f"yT_hi{j}", 64 + 8 * j, [P, KC, TOK], f32r) for j in range(2)]
        yT_lo = [at(f"yT_lo{j}", 68 + 8 * j, [P, KC, TOK], f32r) for j in range(2)]
        ys = [at("ys0", 80, [P, SL, DIM]), at("ys1", 86, [P, SL, DIM])]
        h = at("h", 90, [P, 2, TOK])
        h_hi = at("h_hi", 92, [P, 2, TOK], f32r)
        h_lo = at("h_lo", 94, [P, 2, TOK], f32r)
        raw2 = at("raw2", 96, [P, 2, DIM])

        def bank(name, shape):
            return ctx.enter_context(nc.psum_tensor(name, shape, fp32))

        ps_unit = [bank(f"ps_unit{j}", [P, DIM]) for j in range(2)]
        ps_zT = bank("ps_zT", [P, KC, P])
        ps_s = bank("ps_s", [P, HP, GS, NODES])
        ps_pT = bank("ps_pT", [P, HP, P])
        ps_o = [bank(f"ps_o{g}", [P, DIM]) for g in range(GS)]
        ps_x1 = bank("ps_x1", [P, DIM])
        ps_acc = [ps_s[:, :, :, :].rearrange("p a b c -> p (a b c)"), ps_pT[:, :, :].rearrange("p a b -> p (a b)"),
                  ps_o[0][:, :], ps_o[1][:, :]]

        ident_set = sem("ident_set")
        cols_loaded = sem("cols_loaded")
        rows_loaded = sem("rows_loaded")
        raw_loaded = [sem(f"raw_loaded{m}") for m in range(4)]
        w_hi_ready = sem("w_hi_ready")
        w_ready = sem("w_ready")
        bias_mm = sem("bias_mm")
        bias_ready = sem("bias_ready")
        bvrep_ready = sem("bvrep_ready")
        zeros_set = sem("zeros_set")
        bq_added = sem("bq_added")

        x_loaded = [sem(f"x_loaded{t}") for t in range(SL)]
        xr_loaded = [sem(f"xr_loaded{t}") for t in range(SL)]
        adj_loaded = [sem(f"adj_loaded{j}") for j in range(2)]
        mask_ready = sem("mask_ready")
        stats_ready = sem("stats_ready")
        moments_ready = sem("moments_ready")
        vareps_ready = sem("vareps_ready")
        rstd_ready = sem("rstd_ready")
        z_ready = sem("z_ready")
        zT_done = sem("zT_done")
        zT_hi_ready = sem("zT_hi_ready")
        zT_ready = sem("zT_ready")
        unit_done = sem("unit_done")
        unit_out = sem("unit_out")
        s_done = sem("s_done")
        masked = sem("masked")
        rowmax_ready = sem("rowmax_ready")
        shifted = sem("shifted")
        exp_ready = sem("exp_ready")
        rowsum_ready = sem("rowsum_ready")
        rowrec_ready = sem("rowrec_ready")
        probs_ready = sem("probs_ready")
        pT_done = sem("pT_done")
        pT_ready = sem("pT_ready")
        pv_done = sem("pv_done")
        oT_hi_ready = sem("oT_hi_ready")
        oT_ready = sem("oT_ready")
        o_done = sem("o_done")
        xr_ready = sem("xr_ready")
        x1_ready = sem("x1_ready")
        x1_stored = [sem(f"x1_stored{t}") for t in range(SL)]

        raw1_loaded = [sem(f"raw1_loaded{j}") for j in range(2)]
        w1_hi_ready = sem("w1_hi_ready")
        w1_ready = sem("w1_ready")
        w1_bias_mm = sem("w1_bias_mm")
        w1_bias_ready = sem("w1_bias_ready")
        raw2_loaded = [sem(f"raw2_loaded{j}") for j in range(2)]
        w2_hi_ready = sem("w2_hi_ready")
        w2_ready = sem("w2_ready")
        y_loaded = [[sem(f"y_loaded{j}_{t}") for t in range(SL)] for j in range(2)]
        yb_ready = sem("yb_ready")
        h_done = sem("h_done")
        h_ready = sem("h_ready")
        h_hi_ready = sem("h_hi_ready")
        h_parts_ready = sem("h_parts_ready")
        mlp_done = sem("mlp_done")
        acc_done = sem("acc_done")
        out_ready = sem("out_ready")
        out_stored = [sem(f"out_stored{t}") for t in range(SL)]

        block = ctx.enter_context(nc.Block())

        def first(i):
            return isinstance(i, int) and i == 0

        LN2 = TILES * SL

        @block.sync
        def _(sp):
            def load_x(i, t):
                if not (isinstance(i, int) and i < 1):
                    sp.wait_ge(z_ready, 4 * (i - 1) + t + 1)
                sp.dma_start(xs[:, t, :], x_v[i, t, :, :]).then_inc(x_loaded[t], 16)

            def load_xr(i, t):
                if not first(i):
                    sp.wait_ge(x1_stored[t], 16 * i)
                sp.dma_start(xr[:, t, :], x_v[i, t, :, :]).then_inc(xr_loaded[t], 16)

            def load_adj(i, j):
                for half in range(2):
                    sp.dma_start(adj_b[half * NODES:(half + 1) * NODES, j, :, :], adj_v[i, :, :, :])\
                      .then_inc(adj_loaded[j], 16)

            def store_x1(i, t):
                sp.wait_ge(x1_ready, 4 * i + t + 1)
                sp.dma_start(x1_v[i, t, :, :], xr[:, t, :]).then_inc(x1_stored[t], 16)

            for t in range(SL):
                load_x(0, t)
            for c, dst in ((ln1_g, g1_col), (ln1_b, b1n_col), (bq, bq_col), (bk, bk_col), (bv, bv_col)):
                sp.dma_start(dst[:, :], c).then_inc(cols_loaded, 16)
            for m, w in enumerate((Wq, Wk, Wv, Wo)):
                sp.dma_start(raw[m][:, :, :], chunked(w)).then_inc(raw_loaded[m], 16)
            for c, dst in ((ln2_g, g2_col), (ln2_b, b2n_col), (b1, bh_col)):
                sp.dma_start(dst[:, :], c).then_inc(rows_loaded, 16)
            for c, dst in ((bo, bo_row), (b2, by_row)):
                sp.dma_start(dst[:, :], row(c)).then_inc(rows_loaded, 16)
            load_adj(0, 0)
            load_adj(1, 1)
            for t in range(SL):
                load_xr(0, t)
            for t in range(SL):
                load_x(1, t)
            for t in range(SL):
                load_x(2, t)

            def attention_tile(i, j, more=True, next_x=True):
                sp.wait_ge(mask_ready, i + 1)
                for t in range(SL):
                    if next_x:
                        load_x(i + 3, t)
                    store_x1(i, t)
                    if more and t:
                        load_xr(i + 1, t - 1)
                if more:
                    load_xr(i + 1, SL - 1)
                if next_x or (isinstance(i, int) and i + 2 < TILES):
                    load_adj(i + 2, j)

            with sp.Fori(0, (TILES - 4) // 2) as pair:
                i = 2 * pair
                attention_tile(i, 0)
                attention_tile(i + 1, 1)
            for i in range(TILES - 4, TILES - 1):
                attention_tile(i, i % 2, next_x=i + 3 < TILES)

            sp.wait_ge(unit_done, UNITS * TILES)
            w1_v = W1.rearrange("(c p) n -> c p n", p=P)

            def load_raw1(c):
                if c >= 2:
                    sp.wait_ge(w1_ready, c - 1)
                    sp.wait_ge(w1_bias_mm, c - 1)
                sp.dma_start(raw1[:, c % 2, :], w1_v[c, :, :]).then_inc(raw1_loaded[c % 2], 16)

            def load_y(i, j, t):
                if isinstance(i, int) and i < 2:
                    sp.wait_ge(x1_stored[t], 16 * (i + 1))
                    if i == 0:
                        sp.wait_ge(z_ready, LN2)
                else:
                    sp.wait_ge(out_stored[t], 16 * (i - 1))
                sp.dma_start(ys[j][:, t, :], x1_v[i, t, :, :]).then_inc(y_loaded[j][t], 16)

            for c in range(2):
                load_raw1(c)
            for t in range(SL):
                load_y(0, 0, t)
            last = TILES - 1
            for t in range(SL):
                store_x1(last, t)
                if t < 2:
                    load_raw1(t + 2)
            for t in range(SL):
                sp.wait_ge(x1_stored[t], 16 * TILES)
            w2_v = W2.rearrange("(c p) n -> c p n", p=P)

            def load_raw2(c):
                if c >= 2:
                    sp.wait_ge(w2_ready, c - 1)
                sp.dma_start(raw2[:, c % 2, :], w2_v[c, :, :]).then_inc(raw2_loaded[c % 2], 16)

            sp.wait_ge(mask_ready, TILES)
            for c in range(2):
                load_raw2(c)
            for t in range(SL):
                load_y(1, 1, t)
            for c in range(2, FC):
                load_raw2(c)

            def store_out(i, j, t):
                sp.wait_ge(out_ready, 4 * i + t + 1)
                sp.dma_start(out_v[i, t, :, :], ys[j][:, t, :]).then_inc(out_stored[t], 16)

            def mlp_tile(i, j, more=True):
                for t in range(SL):
                    store_out(i, j, t)
                if more:
                    for t in range(SL):
                        load_y(i + 2, j, t)

            with sp.Fori(0, (TILES - 2) // 2) as pair:
                i = 2 * pair
                mlp_tile(i, 0)
                mlp_tile(i + 1, 1)
            for i in range(TILES - 2, TILES):
                mlp_tile(i, i % 2, more=False)
            for t in range(SL):
                sp.wait_ge(out_stored[t], 16 * TILES)

        @block.gpsimd
        def _(pool):
            pool.memset(ident[:, :], 0.0).then_inc(ident_set, 1)
            pool.memset(neg_half[:, :], -0.5).then_inc(ident_set, 1)
            pool.memset(eps[:, :], EPS).then_inc(ident_set, 1)
            pool.wait_ge(ident_set, 3)
            pool.affine_select(out=ident[:, :], in_=ident[:, :], compare_op=ALU.not_equal, fill=1.0, base=0,
                               pattern=[[-1, P]], channel_multiplier=1).then_inc(ident_set, 1)

            def zero_q(j):
                pool.memset(q_bd[j][:, :, :, :, :], 0.0).then_inc(zeros_set, 1)

            def norm_power(m, slot):
                pool.wait_ge(moments_ready, m + 1)
                pool.tensor_tensor(var_eps[:, slot, :], moments[:, slot, 1:2], eps[:, :], ALU.add)\
                    .then_inc(vareps_ready, 1)
                pool.wait_ge(vareps_ready, m + 1)
                pool.tensor_tensor(rstd[:, slot, :], var_eps[:, slot, :], neg_half[:, :], ALU.pow)\
                    .then_inc(rstd_ready, 1)

            def add_bias(i, t):
                pool.wait_ge(xr_loaded[t], 16 * (i + 1))
                pool.tensor_tensor(xr[:, t, :], xr[:, t, :], bo_row[:, :], ALU.add).then_inc(xr_ready, 1)

            for m in range(SL):
                norm_power(m, m % 2)
            zero_q(0)
            for m in range(SL, 2 * SL + 1):
                norm_power(m, m % 2)
            pool.wait_ge(w_ready, 4 * KC)
            pool.wait_ge(bias_mm, 4)
            zero_q(1)
            pool.wait_ge(bias_ready, 4)

            def attention_tile(i, norms=SL):
                for t in range(SL):
                    if t < norms:
                        norm_power(4 * (i + 2) + t + 1, (t + 1) % 2)
                    add_bias(i, t)

            with pool.Fori(0, (TILES - 4) // 2) as pair:
                i = 2 * pair
                attention_tile(i)
                attention_tile(i + 1)
            attention_tile(TILES - 4)
            attention_tile(TILES - 3, norms=SL - 1)
            attention_tile(TILES - 2, norms=0)
            attention_tile(TILES - 1, norms=0)

            def norm_rows(m, i, j, t):
                norm_power(LN2 + m, t % 2)
                pool.wait_ge(z_ready, LN2 + m + 1)
                pool.tensor_tensor(ys[j][:, t, :], ys[j][:, t, :], by_row[:, :], ALU.add).then_inc(yb_ready, 1)

            for i in range(2):
                for t in range(SL):
                    norm_rows(4 * i + t, i, i, t)
            with pool.Fori(1, TILES // 2) as pair:
                i = 2 * pair
                for j in range(2):
                    for t in range(SL):
                        norm_rows(4 * (i + j) + t, i + j, j, t)

        @block.scalar
        def _(act):
            def cut_hi(w_hi, m, c, g):
                act.activation(w_hi[:, c, :], raw[m][:, c, :], ACT.Copy, scale=g).then_inc(w_hi_ready, 1)

            def out_zT(m, hi, t):
                act.wait_ge(zT_done, m + 1)
                act.activation(hi[:, :, t * P:(t + 1) * P], ps_zT[:, :, :], ACT.Copy).then_inc(zT_hi_ready, 1)

            def out_unit(i, j, u):
                act.wait_ge(unit_done, UNITS * i + u + 1)
                ps = ps_unit[u % 2]
                if u < K0:
                    for e in range(2):
                        rows = slice(e * NODES, (e + 1) * NODES)
                        ins = act.activation(q_bd[j][rows, u, :, e, :],
                                             ps[rows, :].rearrange("p (g q) -> p g q", q=NODES), ACT.Identity,
                                             bias=bq_col[rows, u:u + 1], scale=QSCALE)
                elif u < V0:
                    c = u - K0
                    ins = act.activation(kT[j][:, c, :], ps[:, :], ACT.Identity, bias=bk_col[:, c:c + 1])
                else:
                    ins = act.activation(v[j][:, u - V0, :], ps[:, :], ACT.Copy)
                ins.then_inc(unit_out, 1)

            def out_pT(n):
                act.wait_ge(pT_done, n + 1)
                act.activation(probsT[:, :, :], ps_pT[:, :, :], ACT.Copy).then_inc(pT_ready, 1)

            def out_o(n):
                act.wait_ge(pv_done, n + 1)
                for g in range(GS):
                    act.activation(oT_hi[:, :, g * NODES:(g + 1) * NODES],
                                   ps_o[g][:, 0:HP * NODES].rearrange("p (h q) -> p h q", q=NODES), ACT.Copy)\
                       .then_inc(oT_hi_ready, 1)

            def exps(n):
                act.wait_ge(shifted, n + 1)
                act.activation(probs[:, :, :, :], probs[:, :, :, :], ACT.Exp).then_inc(exp_ready, 1)

            for t in range(SL):
                out_zT(t, zT_hi[0], t)
            act.wait_ge(cols_loaded, 16 * 5)
            for m, w in enumerate((wq_hi, wk_hi, wv_hi, wo_hi)):
                act.wait_ge(raw_loaded[m], 16)
                for c in range(KC):
                    cut_hi(w, m, c, g1_col[:, c:c + 1] if m < 3 else 1.0)
                if m == 0:
                    act.wait_ge(zeros_set, 1)
                else:
                    if m < 3:
                        act.wait_ge(bias_ready, m)
                    for u in range((m - 1) * KC, m * KC):
                        out_unit(0, 0, u)
            for t in range(SL):
                out_zT(SL + t, zT_hi[1], t)
            act.wait_ge(zeros_set, 2)
            exps(0)

            def attention_tile(i, j, project=True, norm=True):
                for t in range(SL):
                    n = 4 * i + t
                    out_pT(n)
                    if project:
                        out_unit(i + 1, 1 - j, 3 * t)
                    out_o(n)
                    if project or t < SL - 1:
                        exps(n + 1)
                    if project:
                        out_unit(i + 1, 1 - j, 3 * t + 1)
                    if norm:
                        out_zT(n + 2 * SL, zT_hi[j], t)
                    if project:
                        out_unit(i + 1, 1 - j, 3 * t + 2)

            def cut_w1(c):
                act.wait_ge(raw1_loaded[c % 2], 16 * (c // 2 + 1))
                act.activation(w1_hi[:, c, :], raw1[:, c % 2, :], ACT.Copy, scale=g2_col[:, c:c + 1])\
                   .then_inc(w1_hi_ready, 1)

            with act.Fori(0, (TILES - 2) // 2) as pair:
                i = 2 * pair
                attention_tile(i, 0)
                attention_tile(i + 1, 1)
            attention_tile(TILES - 2, 0, norm=False)
            act.wait_ge(rows_loaded, 16 * 5)
            act.wait_ge(unit_done, UNITS * TILES)
            for t in range(SL):
                n = 4 * (TILES - 1) + t
                out_pT(n)
                out_o(n)
                if t < SL - 1:
                    exps(n + 1)
                cut_w1(t)
                out_zT(LN2 + t, yT_hi[0], t)

            def cut_w2(c):
                act.wait_ge(raw2_loaded[c % 2], 16 * (c // 2 + 1))
                act.activation(w2_hi[:, c, :], raw2[:, c % 2, :], ACT.Copy).then_inc(w2_hi_ready, 1)

            def gelu(n, c, s):
                act.wait_ge(h_done, n + 1)
                if not (isinstance(n, int) and n < 2):
                    act.wait_ge(h_parts_ready, n - 1)
                act.activation(h[:, s, :], ps_unit[s][:, :], ACT.Gelu, bias=bh_col[:, c:c + 1]).then_inc(h_ready, 1)

            act.wait_ge(o_done, SL * TILES)
            act.wait_ge(w1_ready, KC)
            act.wait_ge(w1_bias_mm, KC)
            cut_w2(0)
            act.wait_ge(w1_bias_ready, 1)
            gelu(0, 0, 0)
            cut_w2(1)
            gelu(1, 1, 1)

            def mlp_tile(i, j, ahead=True, weights=False):
                for c in range(FC):
                    if weights and c + 2 < FC:
                        cut_w2(c + 2)
                    if ahead or c + 2 < FC:
                        gelu(FC * i + c + 2, (c + 2) % FC, c % 2)
                    if ahead and c % 3 == 0 and 0 < c <= 3 * SL:
                        out_zT(LN2 + 4 * (i + 1) + c // 3 - 1, yT_hi[1 - j], c // 3 - 1)

            mlp_tile(0, 0, weights=True)
            with act.Fori(0, (TILES - 2) // 2) as pair:
                i = 2 * pair + 1
                mlp_tile(i, 1)
                mlp_tile(i + 1, 0)
            mlp_tile(TILES - 1, 1, ahead=False)

        @block.vector
        def _(dve):
            def cut_lo(w_hi, w_lo, m, c, g, n):
                dve.wait_ge(w_hi_ready, n + 1)
                dve.scalar_tensor_tensor(out=w_lo[:, c, :], in0=raw[m][:, c, :], scalar=g,
                                         in1=w_hi[:, c, :].bitcast(fp32), op0=ALU.mult, op1=ALU.subtract)\
                   .then_inc(w_ready, 1)

            def row_stats(m, s, rows, behind=None):
                dve.bn_stats(stats[:, s, :], rows).then_inc(stats_ready, 1)
                dve.wait_ge(stats_ready, m + 1)
                if behind is not None:
                    behind()
                dve.bn_aggr(moments[:, s, :], stats[:, s, :]).then_inc(moments_ready, 1)

            def stats_x(i, t, behind=None):
                dve.wait_ge(x_loaded[t], 16 * (i + 1))
                row_stats(4 * i + t, t % 2, xs[:, t, :], behind)

            def normalise(m, s, rows):
                dve.wait_ge(rstd_ready, m + 1)
                if not (isinstance(m, int) and m < 2):
                    dve.wait_ge(zT_done, m - 1)
                dve.tensor_scalar(z[:, s, :], rows, moments[:, s, 0:1], rstd[:, s, 0:1], ALU.subtract, ALU.mult)\
                   .then_inc(z_ready, 1)

            def lo_zT(m, hi, lo, t):
                dve.wait_ge(zT_hi_ready, m + 1)
                cols = slice(t * P, (t + 1) * P)
                dve.tensor_tensor(lo[:, :, cols], ps_zT[:, :, :], hi[:, :, cols].bitcast(fp32), ALU.subtract)\
                   .then_inc(zT_ready, 1)

            def make_mask(i, j):
                if isinstance(i, int):
                    dve.wait_ge(adj_loaded[j], 32 * (i // 2 + 1))
                else:
                    dve.wait_ge(adj_loaded[j], 16 * (i - j) + 32)
                dve.tensor_scalar(mask[:, j, :, :], adj_b[:, j, :, :], KEEP, NEG, ALU.mult, ALU.add)\
                   .then_inc(mask_ready, 1)

            def softmax_front(n, i, j, t):
                dve.wait_ge(s_done, n + 1)
                dve.wait_ge(mask_ready, i + 1)
                m = mask[:, j, GS * t:GS * (t + 1), :].rearrange("p (a g) k -> p a g k", a=1)\
                    .to_broadcast([P, HP, GS, NODES])
                dve.tensor_tensor(probs[:, :, :, :], ps_s[:, :, :, :], m, ALU.min).then_inc(masked, 1)
                dve.wait_ge(masked, n + 1)
                p3 = probs[:, :, :, :].rearrange("p h g k -> p (h g) k")
                dve.tensor_reduce(rowmax[:, :], p3, AX.X, ALU.max).then_inc(rowmax_ready, 1)
                dve.wait_ge(rowmax_ready, n + 1)
                dve.tensor_tensor(p3, p3, spread(rowmax), ALU.subtract).then_inc(shifted, 1)

            def spread(rows):
                return rows[:, :].rearrange("p (h a) -> p h a", a=1).to_broadcast([P, GS * HP, NODES])

            def softmax_back(n):
                dve.wait_ge(exp_ready, n + 1)
                p3 = probs[:, :, :, :].rearrange("p h g k -> p (h g) k")
                dve.tensor_reduce(rowsum[:, :], p3, AX.X, ALU.add).then_inc(rowsum_ready, 1)
                dve.wait_ge(rowsum_ready, n + 1)
                dve.reciprocal(rowrec[:, :], rowsum[:, :]).then_inc(rowrec_ready, 1)
                dve.wait_ge(rowrec_ready, n + 1)
                dve.tensor_tensor(p3, p3, spread(rowrec), ALU.mult).then_inc(probs_ready, 1)

            def lo_o(n):
                for g in range(GS):
                    dve.wait_ge(oT_hi_ready, 2 * n + g + 1)
                    cols = slice(g * NODES, (g + 1) * NODES)
                    ins = dve.tensor_tensor(oT_lo[:, :, cols],
                                            ps_o[g][:, 0:HP * NODES].rearrange("p (h q) -> p h q", q=NODES),
                                            oT_hi[:, :, cols].bitcast(fp32), ALU.subtract)
                ins.then_inc(oT_ready, 1)

            def residual(n, t):
                dve.wait_ge(o_done, n + 1)
                dve.wait_ge(xr_ready, n + 1)
                dve.tensor_tensor(xr[:, t, :], ps_x1[:, :], xr[:, t, :], ALU.add).then_inc(x1_ready, 1)

            stats_x(0, 0)
            for t in range(SL):
                if t < SL - 1:
                    stats_x(0, t + 1)
                normalise(t, t % 2, xs[:, t, :])
                lo_zT(t, zT_hi[0], zT_lo[0], t)
            dve.wait_ge(cols_loaded, 16 * 5)
            n = 0
            for m, (hi, lo) in enumerate(((wq_hi, wq_lo), (wk_hi, wk_lo), (wv_hi, wv_lo), (wo_hi, wo_lo))):
                dve.wait_ge(raw_loaded[m], 16)
                for c in range(KC):
                    cut_lo(hi, lo, m, c, g1_col[:, c:c + 1] if m < 3 else 1.0, n)
                    n += 1
                dve.wait_ge(bias_mm, m + 1)
                if m == 0:
                    dve.tensor_tensor(bq_col[:, :], ps_s[:, 0, 0, 0:KC], bq_col[:, :], ALU.add)\
                       .then_inc(bq_added, 1)
                    dve.wait_ge(bq_added, 1)
                    dve.tensor_scalar(bq_col[:, :], bq_col[:, :], QSCALE, None, ALU.mult).then_inc(bias_ready, 1)
                elif m == 1:
                    dve.tensor_tensor(bk_col[:, :], ps_pT[:, 0, 0:KC], bk_col[:, :], ALU.add).then_inc(bias_ready, 1)
                elif m == 2:
                    dve.tensor_tensor(bv_col[:, :], ps_o[0][:, 0:KC], bv_col[:, :], ALU.add)\
                       .then_inc(bias_ready, 1)
                    dve.wait_ge(bias_ready, 3)
                    dve.tensor_copy(bv_rep[:, :, :], bv_col[:, :].rearrange("p (c a) -> p c a", a=1)
                                    .to_broadcast([P, KC, P])).then_inc(bvrep_ready, 1)
                else:
                    dve.wait_ge(rows_loaded, 16 * 5)
                    dve.tensor_tensor(bo_row[:, :], ps_x1[:, :], bo_row[:, :], ALU.add).then_inc(bias_ready, 1)
            stats_x(1, 0)
            for t in range(SL):
                if t < SL - 1:
                    stats_x(1, t + 1)
                else:
                    stats_x(2, 0)
                normalise(SL + t, t % 2, xs[:, t, :])
                lo_zT(SL + t, zT_hi[1], zT_lo[1], t)
            make_mask(0, 0)
            softmax_front(0, 0, 0, 0)
            softmax_back(0)

            def attention_tile(i, j, project=True, norm=True, more_rows=True):
                for t in range(SL):
                    n = 4 * i + t
                    if norm:
                        def rows_now():
                            normalise(n + 2 * SL, t % 2, xs[:, t, :])

                        if t < SL - 1:
                            stats_x(i + 2, t + 1, rows_now)
                        elif more_rows:
                            stats_x(i + 3, 0, rows_now)
                        else:
                            rows_now()
                    if project or t < SL - 1:
                        if t < SL - 1:
                            softmax_front(n + 1, i, j, t + 1)
                        else:
                            make_mask(i + 1, 1 - j)
                            softmax_front(n + 1, i + 1, 1 - j, 0)
                    lo_o(n)
                    if project or t < SL - 1:
                        softmax_back(n + 1)
                    if norm:
                        lo_zT(n + 2 * SL, zT_hi[j], zT_lo[j], t)
                    residual(n, t)

            with dve.Fori(0, (TILES - 4) // 2) as pair:
                i = 2 * pair
                attention_tile(i, 0)
                attention_tile(i + 1, 1)
            attention_tile(TILES - 4, 0)
            attention_tile(TILES - 3, 1, more_rows=False)
            attention_tile(TILES - 2, 0, norm=False)

            def stats_y(i, j, t, behind=None):
                if isinstance(i, int):
                    dve.wait_ge(y_loaded[j][t], 16 * (i // 2 + 1))
                else:
                    dve.wait_ge(y_loaded[j][t], 8 * (i - j) + 16)
                row_stats(LN2 + 4 * i + t, t % 2, ys[j][:, t, :], behind)

            def normalise_y(i, j, t):
                normalise(LN2 + 4 * i + t, t % 2, ys[j][:, t, :])

            def cut_w1(c):
                dve.wait_ge(raw1_loaded[c % 2], 16 * (c // 2 + 1))
                dve.wait_ge(w1_hi_ready, c + 1)
                dve.scalar_tensor_tensor(out=w1_lo[:, c, :], in0=raw1[:, c % 2, :], scalar=g2_col[:, c:c + 1],
                                         in1=w1_hi[:, c, :].bitcast(fp32), op0=ALU.mult, op1=ALU.subtract)\
                   .then_inc(w1_ready, 1)

            last = TILES - 1
            dve.wait_ge(unit_done, UNITS * TILES)
            dve.wait_ge(rows_loaded, 16 * 5)
            for t in range(SL):
                n = 4 * last + t
                if t < SL - 1:
                    softmax_front(n + 1, last, last % 2, t + 1)
                lo_o(n)
                if t < SL - 1:
                    softmax_back(n + 1)
                cut_w1(t)
                stats_y(0, 0, t)
                normalise_y(0, 0, t)
                lo_zT(LN2 + t, yT_hi[0], yT_lo[0], t)
                residual(n, t)
            dve.wait_ge(w1_bias_mm, KC)
            dve.tensor_tensor(bh_col[:, :], ps_unit[1][:, 0:FC], bh_col[:, :], ALU.add).then_inc(w1_bias_ready, 1)

            def cut_w2(c):
                dve.wait_ge(w2_hi_ready, c + 1)
                dve.tensor_tensor(w2_lo[:, c, :], raw2[:, c % 2, :], w2_hi[:, c, :].bitcast(fp32), ALU.subtract)\
                   .then_inc(w2_ready, 1)

            def cut_h(i, c, s):
                n = FC * i + c
                dve.wait_ge(h_ready, n + 1)
                if c == 1 and not first(i):
                    dve.wait_ge(acc_done, SL * i)
                elif c >= 2 or not first(i):
                    dve.wait_ge(mlp_done, (FC - 1) * i + max(c - 1, 0))
                dve.tensor_copy(h_hi[:, s, :], h[:, s, :]).then_inc(h_hi_ready, 1)
                dve.wait_ge(h_hi_ready, n + 1)
                dve.tensor_tensor(h_lo[:, s, :], h[:, s, :], h_hi[:, s, :].bitcast(fp32), ALU.subtract)\
                   .then_inc(h_parts_ready, 1)

            def finish(i, j, t):
                dve.wait_ge(acc_done, 4 * i + t + 1)
                dve.wait_ge(yb_ready, 4 * i + t + 1)
                dve.tensor_tensor(ys[j][:, t, :], ps_acc[t], ys[j][:, t, :], ALU.add).then_inc(out_ready, 1)

            cut_w2(0)
            cut_h(0, 0, 0)
            cut_w2(1)
            cut_h(0, 1, 1)

            def mlp_tile(i, j, ahead=True, weights=False, before=True):
                for c in range(FC):
                    if weights and c + 2 < FC:
                        cut_w2(c + 2)
                    if c == 0 and before:
                        for t in range(SL):
                            finish(i - 1, 1 - j, t)
                    t = (c - 2) // 3
                    if ahead and c % 3 == 1 and 0 <= t < SL:
                        lo_zT(LN2 + 4 * (i + 1) + t, yT_hi[1 - j], yT_lo[1 - j], t)
                    if ahead and c % 3 == 0 and 0 <= t < SL:
                        normalise_y(i + 1, 1 - j, t)
                    def part():
                        if c + 2 < FC:
                            cut_h(i, c + 2, c % 2)
                        else:
                            cut_h(i + 1, c + 2 - FC, c % 2)

                    if ahead and c % 3 == 2 and t < SL:
                        stats_y(i + 1, 1 - j, t, part)
                    elif ahead or c + 2 < FC:
                        part()

            mlp_tile(0, 0, weights=True, before=False)
            with dve.Fori(0, (TILES - 2) // 2) as pair:
                i = 2 * pair + 1
                mlp_tile(i, 1)
                mlp_tile(i + 1, 0)
            mlp_tile(TILES - 1, 1, ahead=False)
            for t in range(SL):
                finish(TILES - 1, 1, t)

        @block.tensor
        def _(pe):
            def three(ps, lhs_hi, lhs_lo, rhs_hi, rhs_lo, start, stop):
                pe.matmul(ps, lhs_hi, rhs_lo, start=start, stop=False)
                pe.matmul(ps, lhs_lo, rhs_hi, start=False, stop=False)
                return pe.matmul(ps, lhs_hi, rhs_hi, start=False, stop=stop)

            def transpose_rows(m, s):
                pe.wait_ge(z_ready, m + 1)
                if not (isinstance(m, int) and m < 1):
                    pe.wait_ge(zT_ready, m)
                for c in range(KC):
                    ins = pe.transpose(ps_zT[:, c, :], z[:, s, c * P:(c + 1) * P], ident[:, :])
                ins.then_inc(zT_done, 1)

            def unit(i, j, u):
                if u == 0:
                    pe.wait_ge(zT_ready, 4 * (i + 1))
                if not (isinstance(i, int) and UNITS * i + u < 2):
                    pe.wait_ge(unit_out, UNITS * i + u - 1)
                ps = ps_unit[u % 2][:, :]
                for c in range(KC):
                    if u < V0:
                        hi, lo = (wq_hi, wq_lo) if u < K0 else (wk_hi, wk_lo)
                        cols = slice(u % KC * P, (u % KC + 1) * P)
                        ins = three(ps, hi[:, c, cols], lo[:, c, cols], zT_hi[j][:, c, :], zT_lo[j][:, c, :],
                                    c == 0, c == KC - 1)
                    else:
                        rows = slice((u - V0) * P, (u - V0 + 1) * P)
                        ins = three(ps, zT_hi[j][:, c, rows], zT_lo[j][:, c, rows], wv_hi[:, c, :], wv_lo[:, c, :],
                                    c == 0, c == KC - 1)
                ins.then_inc(unit_done, 1)

            def scores(n, i, j, t):
                if t == 0:
                    pe.wait_ge(unit_out, UNITS * i + V0)
                if not (isinstance(n, int) and n < 1):
                    pe.wait_ge(masked, n)
                for g in range(GS):
                    for hp in range(HP):
                        a = GS * t + g
                        ins = pe.matmul(ps_s[:, hp, g, :],
                                        q_bd[j][:, hp, a, :, :].rearrange("p e q -> p (e q)"),
                                        kT[j][:, hp, a * NODES:(a + 1) * NODES], start=True, stop=True)
                ins.then_inc(s_done, 1)

            def transpose_probs(n):
                pe.wait_ge(probs_ready, n + 1)
                for hp in range(HP):
                    ins = pe.transpose(ps_pT[:, hp, :], probs[:, hp, :, :].rearrange("p g k -> p (g k)"), ident[:, :])
                ins.then_inc(pT_done, 1)

            def attend(n, j, t, alone):
                if alone:
                    pe.wait_ge(pT_ready, n + 1)
                for g in range(GS):
                    rows = slice(g * NODES, (g + 1) * NODES)
                    for e in range(2):
                        for hp in range(HP):
                            head = 2 * hp + e
                            ins = pe.matmul(ps_o[g][e * DH:(e + 1) * DH, hp * NODES:(hp + 1) * NODES],
                                            v[j][rows, t, head * DH:(head + 1) * DH],
                                            probsT[rows, hp, e * NODES:(e + 1) * NODES], start=True, stop=True)
                ins.then_inc(pv_done, 1)

            def project_out(n):
                pe.wait_ge(oT_ready, n + 1)
                if not (isinstance(n, int) and n < 1):
                    pe.wait_ge(x1_ready, n)
                for c in range(KC):
                    ins = three(ps_x1[:, :], oT_hi[:, c, :], oT_lo[:, c, :], wo_hi[:, c, :], wo_lo[:, c, :],
                                c == 0, c == KC - 1)
                ins.then_inc(o_done, 1)

            def through(m, dst):
                pe.wait_ge(raw_loaded[m], 16)
                for o in range(KC):
                    for c in range(KC):
                        ins = pe.matmul(dst[:, o:o + 1], raw[m][:, c, o * P:(o + 1) * P], b1n_col[:, c:c + 1],
                                        start=(c == 0), stop=(c == KC - 1))
                ins.then_inc(bias_mm, 1)

            pe.wait_ge(ident_set, 4)
            for t in range(SL):
                transpose_rows(t, t % 2)
            pe.wait_ge(cols_loaded, 16 * 5)
            through(0, ps_s[:, 0, 0, :])
            for u in range(UNITS):
                if u % KC == 0:
                    pe.wait_ge(w_ready, KC * (u // KC + 1))
                unit(0, 0, u)
                if u == 1:
                    through(1, ps_pT[:, 0, :])
                if u == 5:
                    through(2, ps_o[0])
                if u == UNITS - 1:
                    pe.wait_ge(bvrep_ready, 1)
                    pe.wait_ge(raw_loaded[3], 16)
                    for c in range(KC):
                        ins = pe.matmul(ps_x1[:, :], bv_rep[:, c, :], raw[3][:, c, :], start=(c == 0),
                                        stop=(c == KC - 1))
                    ins.then_inc(bias_mm, 1)
            pe.wait_ge(bias_ready, 4)
            for t in range(SL):
                transpose_rows(SL + t, t % 2)
            pe.wait_ge(w_ready, 4 * KC)
            scores(0, 0, 0, 0)

            def attention_tile(i, j, project=True, norm=True, w1_bias=False):
                for t in range(SL):
                    n = 4 * i + t
                    transpose_probs(n)
                    if project:
                        unit(i + 1, 1 - j, 3 * t)
                    if t == 0:
                        pe.wait_ge(unit_out, UNITS * (i + 1))
                    if project or t < SL - 1:
                        pe.wait_ge(pT_ready, n + 1)
                    if t < SL - 1:
                        scores(n + 1, i, j, t + 1)
                    elif project:
                        scores(n + 1, i + 1, 1 - j, 0)
                    attend(n, j, t, alone=not project and t == SL - 1)
                    if project:
                        unit(i + 1, 1 - j, 3 * t + 1)
                    if norm:
                        transpose_rows(n + 2 * SL, t % 2)
                    if project:
                        unit(i + 1, 1 - j, 3 * t + 2)
                    if w1_bias:
                        bias_w1(t)
                        transpose_rows(LN2 + t, t % 2)
                    project_out(n)

            def bias_w1(c):
                pe.wait_ge(raw1_loaded[c % 2], 16 * (c // 2 + 1))
                if c == 0:
                    pe.wait_ge(unit_out, UNITS * TILES)
                for f in range(FC):
                    ins = pe.matmul(ps_unit[1][:, f:f + 1], raw1[:, c % 2, f * P:(f + 1) * P], b2n_col[:, c:c + 1],
                                    start=(c == 0 and f == 0), stop=(c == KC - 1), skip_group_check=True)
                ins.then_inc(w1_bias_mm, 1)

            with pe.Fori(0, (TILES - 2) // 2) as pair:
                i = 2 * pair
                attention_tile(i, 0)
                attention_tile(i + 1, 1)
            attention_tile(TILES - 2, 0, norm=False)
            pe.wait_ge(rows_loaded, 16 * 5)
            attention_tile(TILES - 1, 1, project=False, norm=False, w1_bias=True)

            def hidden(n, c, j, s):
                if not (isinstance(n, int) and n < 2):
                    pe.wait_ge(h_ready, n - 1)
                cols = slice(c * P, (c + 1) * P)
                for k in range(KC):
                    ins = three(ps_unit[s][:, :], w1_hi[:, k, cols], w1_lo[:, k, cols], yT_hi[j][:, k, :],
                                yT_lo[j][:, k, :], k == 0, k == KC - 1)
                ins.then_inc(h_done, 1)

            def down(i, n, c, s, weights):
                pe.wait_ge(h_parts_ready, n + 1)
                if weights:
                    pe.wait_ge(w2_ready, c + 1)
                for t in range(SL):
                    if c == 0 and not first(i):
                        pe.wait_ge(out_ready, 4 * (i - 1) + t + 1)
                    rows = slice(t * P, (t + 1) * P)
                    ins = three(ps_acc[t], h_hi[:, s, rows], h_lo[:, s, rows], w2_hi[:, c, :], w2_lo[:, c, :],
                                c == 0, c == FC - 1)
                    if c == FC - 1:
                        ins.then_inc(acc_done, 1)
                if c < FC - 1:
                    ins.then_inc(mlp_done, 1)

            pe.wait_ge(zT_ready, LN2 + SL)
            pe.wait_ge(w1_ready, KC)
            pe.wait_ge(w1_bias_ready, 1)
            hidden(0, 0, 0, 0)
            hidden(1, 1, 0, 1)

            def mlp_tile(i, j, ahead=True, weights=False):
                for c in range(FC):
                    if c + 2 < FC:
                        hidden(FC * i + c + 2, c + 2, j, c % 2)
                    elif ahead:
                        if c + 2 == FC:
                            pe.wait_ge(zT_ready, LN2 + 4 * (i + 2))
                        hidden(FC * i + c + 2, c + 2 - FC, 1 - j, c % 2)
                    down(i, FC * i + c, c, c % 2, weights)
                    if ahead and c % 3 == 0 and 0 < c <= 3 * SL:
                        transpose_rows(LN2 + 4 * (i + 1) + c // 3 - 1, (c // 3 - 1) % 2)

            mlp_tile(0, 0, weights=True)
            with pe.Fori(0, (TILES - 2) // 2) as pair:
                i = 2 * pair + 1
                mlp_tile(i, 1)
                mlp_tile(i + 1, 0)
            mlp_tile(TILES - 1, 1, ahead=False)


_P = "L0_gnn_"
_INS = ["x", "adj"] + [_P + n for n in ("ln1_g", "ln1_b", "ln2_g", "ln2_b", "Wq", "bq", "Wk", "bk", "Wv", "bv",
                                        "Wo", "bo", "W1", "b1", "W2", "b2")]
_COLUMNS = [_P + n for n in ("ln1_g", "ln1_b", "ln2_g", "ln2_b", "bq", "bk", "bv", "b1")]


def kernel(**inputs):
    import numpy as _np
    import concourse.bacc as _bacc
    from concourse import mybir as _mybir
    from concourse.bass_utils import run_bass_kernel_spmd as _run

    nc = _bacc.Bacc("TRN2", target_bir_lowering=False, num_devices=1)
    arrays, args = {}, []
    for name in _INS:
        a = _np.asarray(inputs[name])
        if name in _COLUMNS:
            a = a.reshape(-1, 128).T
        a = _np.ascontiguousarray(a)
        arrays[f"in_{name}_dram"] = a
        args.append(nc.dram_tensor(f"in_{name}_dram", a.shape, _mybir.dt.from_np(a.dtype), kind="ExternalInput").ap())
    args.append(nc.dram_tensor("out_0_dram", inputs["x"].shape, _mybir.dt.float32, kind="ExternalOutput").ap())
    graph_layer(nc, *args)
    r = _run(nc, [arrays], core_ids=[0])
    return r.results[0]["out_0_dram"]
```

```python
import concourse.bass as bass
from concourse import mybir
from contextlib import ExitStack


def graph_layer(nc: bass.Bass, x, adj, ln1_g, ln1_b, ln2_g, ln2_b, Wq, bq, Wk, bk, Wv, bv, Wo, bo, W1, b1, W2, b2,
                out):
    fp32 = mybir.dt.float32
    f32r = mybir.dt.float32r
    u8 = mybir.dt.uint8
    ALU = mybir.AluOpType
    ACT = mybir.ActivationFunctionType
    AX = mybir.AxisListType

    GRAPHS, NODES, DIM = x.shape
    FF = W1.shape[1]
    HEADS, DH = 8, DIM // 8
    P = 128
    EPS = 1e-5
    NEG = -1.0e9
    KEEP = 3.0e38
    QSCALE = float(DH) ** -0.5

    KC = DIM // P
    HP = HEADS // 2
    FC = FF // P
    GS = P // NODES
    SL = 4
    TOK = SL * P
    GT = TOK // NODES
    TILES = GRAPHS * NODES // TOK
    UNITS = 3 * KC
    Q0, K0, V0 = 0, KC, 2 * KC
    assert UNITS == 3 * SL and TILES % 2 == 0 and TILES >= 6 and HP == KC and GS == 2

    x_v = x.rearrange("a s d -> (a s) d").rearrange("(n t p) d -> n t p d", t=SL, p=P)
    out_v = out.rearrange("a s d -> (a s) d").rearrange("(n t p) d -> n t p d", t=SL, p=P)
    x1_v = nc.dram_tensor("x1_rows", (GRAPHS * NODES, DIM), fp32, kind="Internal").ap()\
        .rearrange("(n t p) d -> n t p d", t=SL, p=P)
    adj_v = adj.rearrange("(n g) q k -> n q g k", g=GT)

    def chunked(w):
        return w.rearrange("(c p) n -> p c n", p=P)

    def row(v):
        return v.rearrange("(a n) -> a n", a=1).to_broadcast([P, v.shape[0]])

    ctx = ExitStack()
    with ctx:
        def keep(name, shape, dt=fp32):
            return ctx.enter_context(nc.sbuf_tensor(name, shape, dt))

        def sem(name):
            return ctx.enter_context(nc.semaphore(name))

        ident = keep("ident", [P, P])
        ones = keep("ones", [P, P])
        g1_col = keep("g1_col", [P, KC])
        b1n_col = keep("b1n_col", [P, KC])
        g2_col = keep("g2_col", [P, KC])
        b2n_col = keep("b2n_col", [P, KC])
        bq_col = keep("bq_col", [P, KC])
        bk_col = keep("bk_col", [P, KC])
        bv_col = keep("bv_col", [P, KC])
        bh_col = keep("bh_col", [P, FC])
        bo_row = keep("bo_row", [P, DIM])
        by_row = keep("by_row", [P, DIM])
        neg_half = keep("neg_half", [P, 1])
        eps = keep("eps", [P, 1])
        stats = keep("stats", [P, 2, 6])
        moments = keep("moments", [P, 2, 2])
        var_eps = keep("var_eps", [P, 2, 1])
        rstd = keep("rstd", [P, 2, 1])
        rowmax = keep("rowmax", [P, GS * HP])
        rowsum = keep("rowsum", [P, GS * HP])
        rowrec = keep("rowrec", [P, GS * HP])

        CH = 4 * DIM
        ARENA = 98 * CH
        arena = ctx.enter_context(nc.sbuf_tensor("arena", [P, ARENA // 4], fp32))
        base = nc.sbuf_base - ARENA

        def at(name, slot, shape, dt=fp32):
            return nc.alloc_sbuf_tensor_at(name, shape, dt, offset=base + int(slot * CH))

        wq_hi = at("wq_hi", 0, [P, KC, DIM], f32r)
        wq_lo = at("wq_lo", 4, [P, KC, DIM], f32r)
        wk_hi = at("wk_hi", 8, [P, KC, DIM], f32r)
        wk_lo = at("wk_lo", 12, [P, KC, DIM], f32r)
        wv_hi = at("wv_hi", 16, [P, KC, DIM], f32r)
        wv_lo = at("wv_lo", 20, [P, KC, DIM], f32r)
        zT_hi = [at(f"zT_hi{j}", 32 - 8 * j, [P, KC, TOK], f32r) for j in range(2)]
        zT_lo = [at(f"zT_lo{j}", 36 - 8 * j, [P, KC, TOK], f32r) for j in range(2)]
        wo_hi = at("wo_hi", 40, [P, KC, DIM], f32r)
        wo_lo = at("wo_lo", 44, [P, KC, DIM], f32r)
        qT = [at(f"qT{j}", 68 - 12 * j, [P, HP, TOK]) for j in range(2)]
        kT = [at(f"kT{j}", 72 - 12 * j, [P, HP, TOK]) for j in range(2)]
        v = [at(f"v{j}", 76 - 12 * j, [P, SL, DIM]) for j in range(2)]
        xs = at("xs", 80, [P, SL, DIM])
        z = at("z", 84, [P, 2, DIM])
        zT = at("zT", 85, [P, KC, P])
        xr = at("xr", 86, [P, SL, DIM])
        probs = at("probs", 90, [P, HP, GS, NODES])
        probsT = at("probsT", 91, [P, HP, P])
        oT_hi = at("oT_hi", 92, [P, HP, P], f32r)
        oT_lo = at("oT_lo", 93, [P, HP, P], f32r)
        mask = at("mask", 94, [P, 2, GT, NODES])
        adj_b = at("adj_b", 96, [P, 2, GT, NODES], u8)
        raw = [at("raw_q", 48, [P, KC, DIM]), at("raw_k", 52, [P, KC, DIM]), at("raw_v", 56, [P, KC, DIM]),
               at("raw_o", 60, [P, KC, DIM])]
        off = at("off", 64, [P, 4, DIM])
        prod = at("prod", 90, [P, KC, DIM])
        w1_hi = at("w1_hi", 0, [P, KC, FF], f32r)
        w1_lo = at("w1_lo", 16, [P, KC, FF], f32r)
        raw1 = [at("raw1_0", 48, [P, FF]), at("raw1_1", 52, [P, FF]), at("raw1_2", 32, [P, FF]),
                at("raw1_3", 36, [P, FF])]
        off1 = at("off1", 97, [P, DIM])
        w2_hi = at("w2_hi", 32, [P, FC, DIM], f32r)
        w2_lo = at("w2_lo", 48, [P, FC, DIM], f32r)
        yT_hi = [at(f"yT_hi{j}", 68 + 8 * j, [P, KC, TOK], f32r) for j in range(2)]
        yT_lo = [at(f"yT_lo{j}", 72 - 8 * j, [P, KC, TOK], f32r) for j in range(2)]
        ys = [at("ys0", 80, [P, SL, DIM]), at("ys1", 86, [P, SL, DIM])]
        h = at("h", 90, [P, 2, TOK])
        h_hi = at("h_hi", 92, [P, 2, TOK], f32r)
        h_lo = at("h_lo", 94, [P, 2, TOK], f32r)
        raw2 = at("raw2", 96, [P, 2, DIM])

        def bank(name, shape):
            return ctx.enter_context(nc.psum_tensor(name, shape, fp32))

        ps_unit = [bank(f"ps_unit{j}", [P, DIM]) for j in range(2)]
        ps_zT = bank("ps_zT", [P, KC, P])
        ps_s = bank("ps_s", [P, HP, GS, NODES])
        ps_pT = bank("ps_pT", [P, HP, P])
        ps_o = [bank(f"ps_o{g}", [P, DIM]) for g in range(GS)]
        ps_x1 = bank("ps_x1", [P, DIM])
        ps_acc = [ps_s[:, :, :, :].rearrange("p a b c -> p (a b c)"), ps_pT[:, :, :].rearrange("p a b -> p (a b)"),
                  ps_o[0][:, :], ps_o[1][:, :]]

        ident_set = sem("ident_set")
        cols_loaded = sem("cols_loaded")
        rows_loaded = sem("rows_loaded")
        raw_loaded = [sem(f"raw_loaded{m}") for m in range(4)]
        w_hi_ready = sem("w_hi_ready")
        w_ready = sem("w_ready")
        bias_mm = sem("bias_mm")
        bias_ready = sem("bias_ready")
        prod_ready = sem("prod_ready")
        prod_halved = sem("prod_halved")
        off_ready = sem("off_ready")
        bq_added = sem("bq_added")

        x_loaded = [sem(f"x_loaded{t}") for t in range(SL)]
        xr_loaded = [sem(f"xr_loaded{t}") for t in range(SL)]
        adj_loaded = [sem(f"adj_loaded{j}") for j in range(2)]
        mask_ready = sem("mask_ready")
        stats_ready = sem("stats_ready")
        moments_ready = sem("moments_ready")
        vareps_ready = sem("vareps_ready")
        rstd_ready = sem("rstd_ready")
        z_ready = sem("z_ready")
        zT_done = sem("zT_done")
        zT_hi_ready = sem("zT_hi_ready")
        zT_ready = sem("zT_ready")
        unit_done = sem("unit_done")
        unit_out = sem("unit_out")
        s_done = sem("s_done")
        masked = sem("masked")
        rowmax_ready = sem("rowmax_ready")
        shifted = sem("shifted")
        exp_ready = sem("exp_ready")
        rowsum_ready = sem("rowsum_ready")
        rowrec_ready = sem("rowrec_ready")
        probs_ready = sem("probs_ready")
        pT_done = sem("pT_done")
        pT_ready = sem("pT_ready")
        pv_done = sem("pv_done")
        oT_hi_ready = sem("oT_hi_ready")
        oT_ready = sem("oT_ready")
        o_done = sem("o_done")
        xr_ready = sem("xr_ready")
        x1_ready = sem("x1_ready")
        x1_stored = [sem(f"x1_stored{t}") for t in range(SL)]

        raw1_loaded = [sem(f"raw1_loaded{c}") for c in range(KC)]
        off1_step = sem("off1_step")
        off1_ready = sem("off1_ready")
        w1_hi_ready = sem("w1_hi_ready")
        w1_ready = sem("w1_ready")
        w1_bias_mm = sem("w1_bias_mm")
        w1_bias_ready = sem("w1_bias_ready")
        raw2_loaded = [sem(f"raw2_loaded{j}") for j in range(2)]
        w2_hi_ready = sem("w2_hi_ready")
        w2_ready = sem("w2_ready")
        y_loaded = [[sem(f"y_loaded{j}_{t}") for t in range(SL)] for j in range(2)]
        yb_ready = sem("yb_ready")
        h_done = sem("h_done")
        h_ready = sem("h_ready")
        h_hi_ready = sem("h_hi_ready")
        h_parts_ready = sem("h_parts_ready")
        mlp_done = sem("mlp_done")
        acc_done = sem("acc_done")
        out_ready = sem("out_ready")
        out_stored = [sem(f"out_stored{t}") for t in range(SL)]

        block = ctx.enter_context(nc.Block())

        def first(i):
            return isinstance(i, int) and i == 0

        LN2 = TILES * SL

        @block.sync
        def _(sp):
            def load_x(i, t):
                if not (isinstance(i, int) and i < 1):
                    sp.wait_ge(z_ready, 4 * (i - 1) + t + 1)
                sp.dma_start(xs[:, t, :], x_v[i, t, :, :]).then_inc(x_loaded[t], 16)

            def load_xr(i, t):
                if not first(i):
                    sp.wait_ge(x1_stored[t], 16 * i)
                sp.dma_start(xr[:, t, :], x_v[i, t, :, :]).then_inc(xr_loaded[t], 16)

            def load_adj(i, j):
                for half in range(2):
                    sp.dma_start(adj_b[half * NODES:(half + 1) * NODES, j, :, :], adj_v[i, :, :, :])\
                      .then_inc(adj_loaded[j], 16)

            def store_x1(i, t):
                sp.wait_ge(x1_ready, 4 * i + t + 1)
                sp.dma_start(x1_v[i, t, :, :], xr[:, t, :]).then_inc(x1_stored[t], 16)

            for t in range(SL):
                load_x(0, t)
            for c, dst in ((ln1_g, g1_col), (ln1_b, b1n_col), (bq, bq_col), (bk, bk_col), (bv, bv_col)):
                sp.dma_start(dst[:, :], c).then_inc(cols_loaded, 16)
            for m, w in enumerate((Wq, Wk, Wv, Wo)):
                sp.dma_start(raw[m][:, :, :], chunked(w)).then_inc(raw_loaded[m], 16)
            for c, dst in ((ln2_g, g2_col), (ln2_b, b2n_col), (b1, bh_col)):
                sp.dma_start(dst[:, :], c).then_inc(rows_loaded, 16)
            for c, dst in ((bo, bo_row), (b2, by_row)):
                sp.dma_start(dst[:, :], row(c)).then_inc(rows_loaded, 16)
            load_adj(0, 0)
            load_adj(1, 1)
            for t in range(SL):
                load_xr(0, t)
            for t in range(SL):
                load_x(1, t)
            for t in range(SL):
                load_x(2, t)

            def attention_tile(i, j, more=True, next_x=True):
                sp.wait_ge(mask_ready, i + 1)
                for t in range(SL):
                    if next_x:
                        load_x(i + 3, t)
                    store_x1(i, t)
                    if more and t:
                        load_xr(i + 1, t - 1)
                if more:
                    load_xr(i + 1, SL - 1)
                if next_x or (isinstance(i, int) and i + 2 < TILES):
                    load_adj(i + 2, j)

            w1_v = W1.rearrange("(c p) n -> c p n", p=P)

            def load_raw1(c):
                sp.dma_start(raw1[c][:, :], w1_v[c, :, :]).then_inc(raw1_loaded[c], 16)

            def load_y(i, j, t):
                if isinstance(i, int) and i < 2:
                    sp.wait_ge(x1_stored[t], 16 * (i + 1))
                    if i == 0:
                        sp.wait_ge(z_ready, LN2)
                else:
                    sp.wait_ge(out_stored[t], 16 * (i - 1))
                sp.dma_start(ys[j][:, t, :], x1_v[i, t, :, :]).then_inc(y_loaded[j][t], 16)

            with sp.Fori(0, (TILES - 4) // 2) as pair:
                i = 2 * pair
                attention_tile(i, 0)
                attention_tile(i + 1, 1)
            attention_tile(TILES - 4, 0)
            sp.wait_ge(w_ready, 4 * KC)
            sp.wait_ge(off_ready, 4)
            for c in range(2):
                load_raw1(c)
            attention_tile(TILES - 3, 1, next_x=False)
            sp.wait_ge(unit_done, UNITS * (TILES - 1))
            for c in range(2, KC):
                load_raw1(c)
            for t in range(SL):
                load_y(0, 0, t)
            attention_tile(TILES - 2, 0, next_x=False)
            for t in range(SL):
                store_x1(TILES - 1, t)
            for t in range(SL):
                sp.wait_ge(x1_stored[t], 16 * TILES)
            w2_v = W2.rearrange("(c p) n -> c p n", p=P)

            def load_raw2(c):
                if c >= 2:
                    sp.wait_ge(w2_ready, c - 1)
                sp.dma_start(raw2[:, c % 2, :], w2_v[c, :, :]).then_inc(raw2_loaded[c % 2], 16)

            sp.wait_ge(mask_ready, TILES)
            sp.wait_ge(w1_bias_mm, 4)
            for c in range(2):
                load_raw2(c)
            for t in range(SL):
                load_y(1, 1, t)
            for c in range(2, FC):
                load_raw2(c)

            def store_out(i, j, t):
                sp.wait_ge(out_ready, 4 * i + t + 1)
                sp.dma_start(out_v[i, t, :, :], ys[j][:, t, :]).then_inc(out_stored[t], 16)

            def mlp_tile(i, j, more=True):
                for t in range(SL):
                    store_out(i, j, t)
                if more:
                    for t in range(SL):
                        load_y(i + 2, j, t)

            with sp.Fori(0, (TILES - 2) // 2) as pair:
                i = 2 * pair
                mlp_tile(i, 0)
                mlp_tile(i + 1, 1)
            for i in range(TILES - 2, TILES):
                mlp_tile(i, i % 2, more=False)
            for t in range(SL):
                sp.wait_ge(out_stored[t], 16 * TILES)

        @block.gpsimd
        def _(pool):
            pool.memset(ident[:, :], 0.0).then_inc(ident_set, 1)
            pool.memset(neg_half[:, :], -0.5).then_inc(ident_set, 1)
            pool.memset(eps[:, :], EPS).then_inc(ident_set, 1)
            pool.memset(ones[:, :], 1.0).then_inc(ident_set, 1)
            pool.wait_ge(ident_set, 4)
            pool.affine_select(out=ident[:, :], in_=ident[:, :], compare_op=ALU.not_equal, fill=1.0, base=0,
                               pattern=[[-1, P]], channel_multiplier=1).then_inc(ident_set, 1)

            def add_chunks(m):
                pool.wait_ge(prod_ready, KC * (m + 1))
                pool.tensor_tensor(prod[:, 0:2, :], prod[:, 0:2, :], prod[:, 2:4, :], ALU.add).then_inc(prod_halved, 1)
                pool.wait_ge(prod_halved, m + 1)
                pool.tensor_tensor(off[:, m, :], prod[:, 0, :], prod[:, 1, :], ALU.add).then_inc(off_ready, 1)

            def norm_power(m, slot):
                pool.wait_ge(moments_ready, m + 1)
                pool.tensor_tensor(var_eps[:, slot, :], moments[:, slot, 1:2], eps[:, :], ALU.add)\
                    .then_inc(vareps_ready, 1)
                pool.wait_ge(vareps_ready, m + 1)
                pool.tensor_tensor(rstd[:, slot, :], var_eps[:, slot, :], neg_half[:, :], ALU.pow)\
                    .then_inc(rstd_ready, 1)

            def add_bias(i, t):
                pool.wait_ge(xr_loaded[t], 16 * (i + 1))
                pool.tensor_tensor(xr[:, t, :], xr[:, t, :], bo_row[:, :], ALU.add).then_inc(xr_ready, 1)

            for m in range(SL):
                norm_power(m, m % 2)
            for m in range(4):
                add_chunks(m)
            for m in range(SL, 2 * SL + 1):
                norm_power(m, m % 2)
            pool.wait_ge(bias_ready, 4)

            def attention_tile(i, norms=SL):
                for t in range(SL):
                    if t < norms:
                        norm_power(4 * (i + 2) + t + 1, (t + 1) % 2)
                    add_bias(i, t)

            with pool.Fori(0, (TILES - 4) // 2) as pair:
                i = 2 * pair
                attention_tile(i)
                attention_tile(i + 1)
            attention_tile(TILES - 4)
            attention_tile(TILES - 3, norms=SL - 1)
            attention_tile(TILES - 2, norms=0)

            def norm_rows(m, i, j, t):
                norm_power(LN2 + m, t % 2)
                pool.wait_ge(z_ready, LN2 + m + 1)
                pool.tensor_tensor(ys[j][:, t, :], ys[j][:, t, :], by_row[:, :], ALU.add).then_inc(yb_ready, 1)

            pool.wait_ge(rows_loaded, 16 * 5)
            for t in range(SL):
                add_bias(TILES - 1, t)
                norm_rows(t, 0, 0, t)
            for t in range(SL):
                norm_rows(4 + t, 1, 1, t)
            with pool.Fori(1, TILES // 2) as pair:
                i = 2 * pair
                for j in range(2):
                    for t in range(SL):
                        norm_rows(4 * (i + j) + t, i + j, j, t)

        @block.scalar
        def _(act):
            def cut_hi(w_hi, m, c, g):
                act.activation(w_hi[:, c, :], raw[m][:, c, :], ACT.Copy, scale=g).then_inc(w_hi_ready, 1)

            def out_zT(m, src, hi, t):
                act.wait_ge(zT_done, m + 1)
                act.activation(hi[:, :, t * P:(t + 1) * P], src[:, :, :], ACT.Copy).then_inc(zT_hi_ready, 1)

            def out_unit(i, j, u):
                act.wait_ge(unit_done, UNITS * i + u + 1)
                ps = ps_unit[u % 2]
                if u < K0:
                    ins = act.activation(qT[j][:, u, :], ps[:, :], ACT.Identity, bias=bq_col[:, u:u + 1],
                                         scale=QSCALE)
                elif u < V0:
                    c = u - K0
                    ins = act.activation(kT[j][:, c, :], ps[:, :], ACT.Identity, bias=bk_col[:, c:c + 1])
                else:
                    ins = act.activation(v[j][:, u - V0, :], ps[:, :], ACT.Copy)
                ins.then_inc(unit_out, 1)

            def out_pT(n):
                act.wait_ge(pT_done, n + 1)
                act.activation(probsT[:, :, :], ps_pT[:, :, :], ACT.Copy).then_inc(pT_ready, 1)

            def out_o(n):
                act.wait_ge(pv_done, n + 1)
                for g in range(GS):
                    act.activation(oT_hi[:, :, g * NODES:(g + 1) * NODES],
                                   ps_o[g][:, 0:HP * NODES].rearrange("p (h q) -> p h q", q=NODES), ACT.Copy)\
                       .then_inc(oT_hi_ready, 1)

            def exps(n):
                act.wait_ge(shifted, n + 1)
                act.activation(probs[:, :, :, :], probs[:, :, :, :], ACT.Exp).then_inc(exp_ready, 1)

            for t in range(SL):
                out_zT(t, ps_zT, zT_hi[0], t)
            act.wait_ge(cols_loaded, 16 * 5)

            def cut(k):
                m, c = k // KC, k % KC
                if c == 0:
                    act.wait_ge(raw_loaded[m], 16)
                cut_hi((wq_hi, wk_hi, wv_hi, wo_hi)[m], m, c, g1_col[:, c:c + 1] if m < 3 else 1.0)

            def weigh(m):
                if m:
                    act.wait_ge(off_ready, m)
                for c in range(KC):
                    act.activation(prod[:, c, :], raw[m][:, c, :], ACT.Copy,
                                   scale=(b1n_col if m < 3 else bv_col)[:, c:c + 1]).then_inc(prod_ready, 1)

            for k in range(2 * KC):
                cut(k)
                if k == KC - 1:
                    weigh(0)
            weigh(1)
            for u in range(UNITS):
                if u == 0 or u == K0:
                    act.wait_ge(bias_ready, 1 + u // KC)
                out_unit(0, 0, u)
                if u < 2 * KC:
                    cut(2 * KC + u)
                if u == 2:
                    act.wait_ge(raw_loaded[2], 16)
                    weigh(2)
                if u == 7:
                    act.wait_ge(bias_ready, 3)
                    weigh(3)
                if u >= V0:
                    out_zT(SL + u - V0, zT, zT_hi[1], u - V0)
            exps(0)
            act.wait_ge(bias_ready, 4)

            def attention_tile(i, j, project=True, norm=True):
                for t in range(SL):
                    n = 4 * i + t
                    out_pT(n)
                    if project:
                        out_unit(i + 1, 1 - j, 3 * t)
                    out_o(n)
                    if project or t < SL - 1:
                        exps(n + 1)
                    if project:
                        out_unit(i + 1, 1 - j, 3 * t + 1)
                    if norm:
                        out_zT(n + 2 * SL, zT, zT_hi[j], t)
                    if project:
                        out_unit(i + 1, 1 - j, 3 * t + 2)

            def cut_w1(c):
                act.wait_ge(raw1_loaded[c], 16)
                act.activation(w1_hi[:, c, :], raw1[c][:, :], ACT.Copy, scale=g2_col[:, c:c + 1])\
                   .then_inc(w1_hi_ready, 1)

            with act.Fori(0, (TILES - 2) // 2) as pair:
                i = 2 * pair
                attention_tile(i, 0)
                attention_tile(i + 1, 1)
            attention_tile(TILES - 2, 0, norm=False)
            act.wait_ge(rows_loaded, 16 * 5)
            act.wait_ge(unit_done, UNITS * TILES)
            for t in range(SL):
                n = 4 * (TILES - 1) + t
                out_pT(n)
                out_o(n)
                if t < SL - 1:
                    exps(n + 1)
                out_zT(LN2 + t, ps_zT, yT_hi[0], t)
                cut_w1(t)

            def cut_w2(c):
                act.wait_ge(raw2_loaded[c % 2], 16 * (c // 2 + 1))
                act.activation(w2_hi[:, c, :], raw2[:, c % 2, :], ACT.Copy).then_inc(w2_hi_ready, 1)

            def gelu(n, c, s):
                act.wait_ge(h_done, n + 1)
                if not (isinstance(n, int) and n < 2):
                    act.wait_ge(h_parts_ready, n - 1)
                act.activation(h[:, s, :], ps_unit[s][:, :], ACT.Gelu, bias=bh_col[:, c:c + 1]).then_inc(h_ready, 1)

            act.wait_ge(o_done, SL * TILES)
            act.wait_ge(w1_ready, KC)
            cut_w2(0)
            act.wait_ge(w1_bias_ready, 1)
            gelu(0, 0, 0)
            cut_w2(1)
            gelu(1, 1, 1)

            def mlp_tile(i, j, ahead=True, weights=False):
                for c in range(FC):
                    if weights and c + 2 < FC:
                        cut_w2(c + 2)
                    if ahead or c + 2 < FC:
                        gelu(FC * i + c + 2, (c + 2) % FC, c % 2)
                    if ahead and c % 3 == 0 and 0 < c <= 3 * SL:
                        out_zT(LN2 + 4 * (i + 1) + c // 3 - 1, zT, yT_hi[1 - j], c // 3 - 1)

            mlp_tile(0, 0, weights=True)
            with act.Fori(0, (TILES - 2) // 2) as pair:
                i = 2 * pair + 1
                mlp_tile(i, 1)
                mlp_tile(i + 1, 0)
            mlp_tile(TILES - 1, 1, ahead=False)

        @block.vector
        def _(dve):
            def cut_lo(w_hi, w_lo, m, c, g, n):
                dve.wait_ge(w_hi_ready, n + 1)
                dve.scalar_tensor_tensor(out=w_lo[:, c, :], in0=raw[m][:, c, :], scalar=g,
                                         in1=w_hi[:, c, :].bitcast(fp32), op0=ALU.mult, op1=ALU.subtract)\
                   .then_inc(w_ready, 1)

            def row_stats(m, s, rows, behind=None):
                dve.bn_stats(stats[:, s, :], rows).then_inc(stats_ready, 1)
                dve.wait_ge(stats_ready, m + 1)
                if behind is not None:
                    behind()
                dve.bn_aggr(moments[:, s, :], stats[:, s, :]).then_inc(moments_ready, 1)

            def stats_x(i, t, behind=None):
                dve.wait_ge(x_loaded[t], 16 * (i + 1))
                row_stats(4 * i + t, t % 2, xs[:, t, :], behind)

            def normalise(m, s, rows, alternate=False):
                dve.wait_ge(rstd_ready, m + 1)
                if not (isinstance(m, int) and m < 2):
                    dve.wait_ge(zT_done, m - 1 if alternate else m)
                dve.tensor_scalar(z[:, s if alternate else 0, :], rows, moments[:, s, 0:1], rstd[:, s, 0:1], ALU.subtract, ALU.mult)\
                   .then_inc(z_ready, 1)

            def turn(m):
                dve.wait_ge(z_ready, m + 1)
                rows = z[:, 0, :].rearrange("p (c f) -> p c f", f=P)
                for a in range(0, P, 32):
                    for b in range(0, P, 32):
                        ins = dve.transpose(zT[b:b + 32, :, a:a + 32], rows[a:a + 32, :, b:b + 32])
                ins.then_inc(zT_done, 1)

            def lo_zT(m, src, hi, lo, t):
                dve.wait_ge(zT_hi_ready, m + 1)
                cols = slice(t * P, (t + 1) * P)
                dve.tensor_tensor(lo[:, :, cols], src[:, :, :], hi[:, :, cols].bitcast(fp32), ALU.subtract)\
                   .then_inc(zT_ready, 1)

            def make_mask(i, j):
                if isinstance(i, int):
                    dve.wait_ge(adj_loaded[j], 32 * (i // 2 + 1))
                else:
                    dve.wait_ge(adj_loaded[j], 16 * (i - j) + 32)
                dve.tensor_scalar(mask[:, j, :, :], adj_b[:, j, :, :], KEEP, NEG, ALU.mult, ALU.add)\
                   .then_inc(mask_ready, 1)

            def softmax_front(n, i, j, t):
                dve.wait_ge(s_done, n + 1)
                dve.wait_ge(mask_ready, i + 1)
                m = mask[:, j, GS * t:GS * (t + 1), :].rearrange("p (a g) k -> p a g k", a=1)\
                    .to_broadcast([P, HP, GS, NODES])
                dve.tensor_tensor(probs[:, :, :, :], ps_s[:, :, :, :], m, ALU.min).then_inc(masked, 1)
                dve.wait_ge(masked, n + 1)
                p3 = probs[:, :, :, :].rearrange("p h g k -> p (h g) k")
                dve.tensor_reduce(rowmax[:, :], p3, AX.X, ALU.max).then_inc(rowmax_ready, 1)
                dve.wait_ge(rowmax_ready, n + 1)
                dve.tensor_tensor(p3, p3, spread(rowmax), ALU.subtract).then_inc(shifted, 1)

            def spread(rows):
                return rows[:, :].rearrange("p (h a) -> p h a", a=1).to_broadcast([P, GS * HP, NODES])

            def softmax_back(n):
                dve.wait_ge(exp_ready, n + 1)
                p3 = probs[:, :, :, :].rearrange("p h g k -> p (h g) k")
                dve.tensor_reduce(rowsum[:, :], p3, AX.X, ALU.add).then_inc(rowsum_ready, 1)
                dve.wait_ge(rowsum_ready, n + 1)
                dve.reciprocal(rowrec[:, :], rowsum[:, :]).then_inc(rowrec_ready, 1)
                dve.wait_ge(rowrec_ready, n + 1)
                dve.tensor_tensor(p3, p3, spread(rowrec), ALU.mult).then_inc(probs_ready, 1)

            def lo_o(n):
                for g in range(GS):
                    dve.wait_ge(oT_hi_ready, 2 * n + g + 1)
                    cols = slice(g * NODES, (g + 1) * NODES)
                    ins = dve.tensor_tensor(oT_lo[:, :, cols],
                                            ps_o[g][:, 0:HP * NODES].rearrange("p (h q) -> p h q", q=NODES),
                                            oT_hi[:, :, cols].bitcast(fp32), ALU.subtract)
                ins.then_inc(oT_ready, 1)

            def residual(n, t):
                dve.wait_ge(o_done, n + 1)
                dve.wait_ge(xr_ready, n + 1)
                dve.tensor_tensor(xr[:, t, :], ps_x1[:, :], xr[:, t, :], ALU.add).then_inc(x1_ready, 1)

            stats_x(0, 0)
            stats_x(0, 1)
            for t in range(SL):
                normalise(t, t % 2, xs[:, t, :], alternate=True)
                if t + 2 < SL:
                    stats_x(0, t + 2)
                if t:
                    lo_zT(t - 1, ps_zT, zT_hi[0], zT_lo[0], t - 1)
            lo_zT(SL - 1, ps_zT, zT_hi[0], zT_lo[0], SL - 1)
            dve.wait_ge(cols_loaded, 16 * 5)
            for k in range(4 * KC):
                m, c = k // KC, k % KC
                if c == 0:
                    dve.wait_ge(raw_loaded[m], 16)
                hi, lo = ((wq_hi, wq_lo), (wk_hi, wk_lo), (wv_hi, wv_lo), (wo_hi, wo_lo))[m]
                cut_lo(hi, lo, m, c, g1_col[:, c:c + 1] if m < 3 else 1.0, k)
                if k == 2 * KC - 1:
                    dve.wait_ge(bias_mm, 1)
                    dve.tensor_tensor(bq_col[:, :], ps_s[:, 0, 0, 0:KC], bq_col[:, :], ALU.add)\
                       .then_inc(bq_added, 1)
                    dve.wait_ge(bq_added, 1)
                    dve.tensor_scalar(bq_col[:, :], bq_col[:, :], QSCALE, None, ALU.mult).then_inc(bias_ready, 1)
                    dve.wait_ge(bias_mm, 2)
                    dve.tensor_tensor(bk_col[:, :], ps_pT[:, 0, 0:KC], bk_col[:, :], ALU.add).then_inc(bias_ready, 1)
                if k == 3 * KC - 1:
                    dve.wait_ge(bias_mm, 3)
                    dve.tensor_tensor(bv_col[:, :], ps_o[0][:, 0:KC], bv_col[:, :], ALU.add)\
                       .then_inc(bias_ready, 1)
            stats_x(1, 0)
            for t in range(SL):
                if t < SL - 1:
                    stats_x(1, t + 1)
                else:
                    stats_x(2, 0)
                normalise(SL + t, t % 2, xs[:, t, :])
                turn(SL + t)
                lo_zT(SL + t, zT, zT_hi[1], zT_lo[1], t)
            make_mask(0, 0)
            softmax_front(0, 0, 0, 0)
            softmax_back(0)
            dve.wait_ge(rows_loaded, 16 * 5)
            dve.wait_ge(bias_mm, 4)
            dve.tensor_tensor(bo_row[:, :], ps_x1[:, :], bo_row[:, :], ALU.add).then_inc(bias_ready, 1)

            def weigh_w1(t):
                if t:
                    dve.wait_ge(w1_bias_mm, t)
                quarter = slice(t * DIM, (t + 1) * DIM)
                dve.tensor_scalar(off1[:, :], raw1[0][:, quarter], b2n_col[:, 0:1], None, ALU.mult)\
                   .then_inc(off1_step, 1)
                for c in range(1, KC):
                    dve.wait_ge(off1_step, (KC - 1) * t + c)
                    dve.scalar_tensor_tensor(out=off1[:, :], in0=raw1[c][:, quarter], scalar=b2n_col[:, c:c + 1],
                                             in1=off1[:, :], op0=ALU.mult, op1=ALU.add)\
                       .then_inc(off1_ready if c == KC - 1 else off1_step, 1)

            def attention_tile(i, j, project=True, norm=True, more_rows=True, w1_bias=False):
                for t in range(SL):
                    n = 4 * i + t
                    if norm:
                        def rows_now():
                            normalise(n + 2 * SL, t % 2, xs[:, t, :])

                        if t < SL - 1:
                            stats_x(i + 2, t + 1, rows_now)
                        elif more_rows:
                            stats_x(i + 3, 0, rows_now)
                        else:
                            rows_now()
                        turn(n + 2 * SL)
                    if project or t < SL - 1:
                        if t < SL - 1:
                            softmax_front(n + 1, i, j, t + 1)
                        else:
                            make_mask(i + 1, 1 - j)
                            softmax_front(n + 1, i + 1, 1 - j, 0)
                    lo_o(n)
                    if project or t < SL - 1:
                        softmax_back(n + 1)
                    if norm:
                        lo_zT(n + 2 * SL, zT, zT_hi[j], zT_lo[j], t)
                    if w1_bias:
                        weigh_w1(t)
                    residual(n, t)

            with dve.Fori(0, (TILES - 4) // 2) as pair:
                i = 2 * pair
                attention_tile(i, 0)
                attention_tile(i + 1, 1)
            attention_tile(TILES - 4, 0)
            attention_tile(TILES - 3, 1, more_rows=False)
            dve.wait_ge(rows_loaded, 16 * 5)
            for c in range(KC):
                dve.wait_ge(raw1_loaded[c], 16)
            attention_tile(TILES - 2, 0, norm=False, w1_bias=True)

            def stats_y(i, j, t, behind=None):
                if isinstance(i, int):
                    dve.wait_ge(y_loaded[j][t], 16 * (i // 2 + 1))
                else:
                    dve.wait_ge(y_loaded[j][t], 8 * (i - j) + 16)
                row_stats(LN2 + 4 * i + t, t % 2, ys[j][:, t, :], behind)

            def cut_w1(c):
                dve.wait_ge(w1_hi_ready, c + 1)
                dve.scalar_tensor_tensor(out=w1_lo[:, c, :], in0=raw1[c][:, :], scalar=g2_col[:, c:c + 1],
                                         in1=w1_hi[:, c, :].bitcast(fp32), op0=ALU.mult, op1=ALU.subtract)\
                   .then_inc(w1_ready, 1)

            last = TILES - 1
            dve.wait_ge(w1_bias_mm, 4)
            dve.tensor_tensor(bh_col[:, :], ps_zT[:, 0, 0:FC], bh_col[:, :], ALU.add).then_inc(w1_bias_ready, 1)
            for t in range(SL):
                n = 4 * last + t
                stats_y(0, 0, t)
                if t < SL - 1:
                    softmax_front(n + 1, last, last % 2, t + 1)
                normalise(LN2 + t, t % 2, ys[0][:, t, :], alternate=True)
                lo_o(n)
                if t < SL - 1:
                    softmax_back(n + 1)
                lo_zT(LN2 + t, ps_zT, yT_hi[0], yT_lo[0], t)
                residual(n, t)
                cut_w1(t)

            def cut_w2(c):
                dve.wait_ge(w2_hi_ready, c + 1)
                dve.tensor_tensor(w2_lo[:, c, :], raw2[:, c % 2, :], w2_hi[:, c, :].bitcast(fp32), ALU.subtract)\
                   .then_inc(w2_ready, 1)

            def cut_h(i, c, s):
                n = FC * i + c
                dve.wait_ge(h_ready, n + 1)
                if c == 1 and not first(i):
                    dve.wait_ge(acc_done, SL * i)
                elif c >= 2 or not first(i):
                    dve.wait_ge(mlp_done, (FC - 1) * i + max(c - 1, 0))
                dve.tensor_copy(h_hi[:, s, :], h[:, s, :]).then_inc(h_hi_ready, 1)
                dve.wait_ge(h_hi_ready, n + 1)
                dve.tensor_tensor(h_lo[:, s, :], h[:, s, :], h_hi[:, s, :].bitcast(fp32), ALU.subtract)\
                   .then_inc(h_parts_ready, 1)

            def finish(i, j, t):
                dve.wait_ge(acc_done, 4 * i + t + 1)
                dve.wait_ge(yb_ready, 4 * i + t + 1)
                dve.tensor_tensor(ys[j][:, t, :], ps_acc[t], ys[j][:, t, :], ALU.add).then_inc(out_ready, 1)

            cut_w2(0)
            cut_h(0, 0, 0)
            cut_w2(1)
            cut_h(0, 1, 1)

            def mlp_tile(i, j, ahead=True, weights=False, before=True):
                for c in range(FC):
                    if weights and c + 2 < FC:
                        cut_w2(c + 2)
                    if c == 0 and before:
                        for t in range(SL):
                            finish(i - 1, 1 - j, t)
                    t = (c - 2) // 3
                    if ahead and c % 3 == 1 and 0 <= t < SL:
                        lo_zT(LN2 + 4 * (i + 1) + t, zT, yT_hi[1 - j], yT_lo[1 - j], t)
                    turned = c // 3 - 1
                    if ahead and c % 3 == 0 and 0 <= turned < SL:
                        normalise(LN2 + 4 * (i + 1) + turned, turned % 2, ys[1 - j][:, turned, :])
                    def part():
                        if c + 2 < FC:
                            cut_h(i, c + 2, c % 2)
                        else:
                            cut_h(i + 1, c + 2 - FC, c % 2)

                    if ahead and c % 3 == 2 and t < SL:
                        stats_y(i + 1, 1 - j, t, part)
                    elif ahead or c + 2 < FC:
                        part()
                    if ahead and c % 3 == 0 and 0 <= turned < SL:
                        turn(LN2 + 4 * (i + 1) + turned)

            mlp_tile(0, 0, weights=True, before=False)
            with dve.Fori(0, (TILES - 2) // 2) as pair:
                i = 2 * pair + 1
                mlp_tile(i, 1)
                mlp_tile(i + 1, 0)
            mlp_tile(TILES - 1, 1, ahead=False)
            for t in range(SL):
                finish(TILES - 1, 1, t)

        @block.tensor
        def _(pe):
            def three(ps, lhs_hi, lhs_lo, rhs_hi, rhs_lo, start, stop):
                pe.matmul(ps, lhs_hi, rhs_lo, start=start, stop=False)
                pe.matmul(ps, lhs_lo, rhs_hi, start=False, stop=False)
                return pe.matmul(ps, lhs_hi, rhs_hi, start=False, stop=stop)

            def transpose_rows(m, s):
                pe.wait_ge(z_ready, m + 1)
                if not (isinstance(m, int) and m < 1):
                    pe.wait_ge(zT_ready, m)
                for c in range(KC):
                    ins = pe.transpose(ps_zT[:, c, :], z[:, s, c * P:(c + 1) * P], ident[:, :])
                ins.then_inc(zT_done, 1)

            def unit(i, j, u, behind=None):
                if u == 0:
                    pe.wait_ge(zT_ready, 4 * (i + 1))
                if not (isinstance(i, int) and UNITS * i + u < 2):
                    pe.wait_ge(unit_out, UNITS * i + u - 1)
                ps = ps_unit[u % 2][:, :]
                for c in range(KC):
                    if c == KC - 1 and behind is not None:
                        behind()
                    if u < V0:
                        hi, lo = (wq_hi, wq_lo) if u < K0 else (wk_hi, wk_lo)
                        cols = slice(u % KC * P, (u % KC + 1) * P)
                        ins = three(ps, hi[:, c, cols], lo[:, c, cols], zT_hi[j][:, c, :], zT_lo[j][:, c, :],
                                    c == 0, c == KC - 1)
                    else:
                        rows = slice((u - V0) * P, (u - V0 + 1) * P)
                        ins = three(ps, zT_hi[j][:, c, rows], zT_lo[j][:, c, rows], wv_hi[:, c, :], wv_lo[:, c, :],
                                    c == 0, c == KC - 1)
                ins.then_inc(unit_done, 1)

            def await_scores(n, i, t):
                if t == 0:
                    pe.wait_ge(unit_out, UNITS * i + V0)
                if not (isinstance(n, int) and n < 1):
                    pe.wait_ge(masked, n)

            def scores(n, j, t):
                for g in range(GS):
                    tokens = slice((GS * t + g) * NODES, (GS * t + g + 1) * NODES)
                    for hp in range(HP):
                        for e in range(2):
                            rows = slice(e * DH, (e + 1) * DH)
                            ins = pe.matmul(ps_s[rows, hp, g, :], qT[j][rows, hp, tokens], kT[j][rows, hp, tokens],
                                            start=True, stop=True)
                ins.then_inc(s_done, 1)

            def transpose_probs(n):
                pe.wait_ge(probs_ready, n + 1)
                for hp in range(HP):
                    ins = pe.transpose(ps_pT[:, hp, :], probs[:, hp, :, :].rearrange("p g k -> p (g k)"), ident[:, :])
                ins.then_inc(pT_done, 1)

            def await_attend(n, i, t):
                if t == 0:
                    pe.wait_ge(unit_out, UNITS * (i + 1))
                pe.wait_ge(pT_ready, n + 1)

            def attend(n, j, t):
                for g in range(GS):
                    rows = slice(g * NODES, (g + 1) * NODES)
                    for e in range(2):
                        for hp in range(HP):
                            head = 2 * hp + e
                            ins = pe.matmul(ps_o[g][e * DH:(e + 1) * DH, hp * NODES:(hp + 1) * NODES],
                                            v[j][rows, t, head * DH:(head + 1) * DH],
                                            probsT[rows, hp, e * NODES:(e + 1) * NODES], start=True, stop=True)
                ins.then_inc(pv_done, 1)

            def project_out(n):
                pe.wait_ge(oT_ready, n + 1)
                if not (isinstance(n, int) and n < 1):
                    pe.wait_ge(x1_ready, n)
                for c in range(KC):
                    ins = three(ps_x1[:, :], oT_hi[:, c, :], oT_lo[:, c, :], wo_hi[:, c, :], wo_lo[:, c, :],
                                c == 0, c == KC - 1)
                ins.then_inc(o_done, 1)

            def bias_column(m, dst):
                pe.wait_ge(off_ready, m + 1)
                for o in range(KC):
                    ins = pe.matmul(dst[:, o:o + 1], off[:, m, o * P:(o + 1) * P], ones[:, 0:1], start=True,
                                    stop=True)
                ins.then_inc(bias_mm, 1)

            pe.wait_ge(ident_set, 5)
            for t in range(SL):
                transpose_rows(t, t % 2)
            for u in range(UNITS):
                if u % KC == 0:
                    pe.wait_ge(w_ready, KC * (u // KC + 1))
                unit(0, 0, u)
                if u == 0:
                    bias_column(0, ps_s[:, 0, 0, :])
                if u == 1:
                    bias_column(1, ps_pT[:, 0, :])
                if u == 5:
                    bias_column(2, ps_o[0])
                if u == 8:
                    pe.wait_ge(bias_ready, 1)
                    await_scores(0, 0, 0)
                    scores(0, 0, 0)
                if u == UNITS - 1:
                    pe.wait_ge(off_ready, 4)
                    pe.matmul(ps_x1[:, :], ones[:, :], off[:, 3, :], start=True, stop=True).then_inc(bias_mm, 1)
            pe.wait_ge(bias_ready, 4)
            pe.wait_ge(w_ready, 4 * KC)

            def attention_tile(i, j, project=True, w1_bias=False, y_rows=False):
                for t in range(SL):
                    n = 4 * i + t

                    def awaits():
                        if t < SL - 1:
                            await_scores(n + 1, i, t + 1)
                        elif project:
                            await_scores(n + 1, i + 1, 0)
                        await_attend(n, i, t)

                    transpose_probs(n)
                    if project:
                        unit(i + 1, 1 - j, 3 * t, awaits)
                    elif t < SL - 1:
                        await_scores(n + 1, i, t + 1)
                    if t < SL - 1:
                        scores(n + 1, j, t + 1)
                    elif project:
                        scores(n + 1, 1 - j, 0)
                    if not project:
                        await_attend(n, i, t)
                    attend(n, j, t)
                    if project:
                        unit(i + 1, 1 - j, 3 * t + 1)
                        unit(i + 1, 1 - j, 3 * t + 2)
                    if w1_bias:
                        bias_w1(t)
                    if y_rows:
                        transpose_rows(LN2 + t, t % 2)
                    project_out(n)

            def bias_w1(t):
                pe.wait_ge(off1_ready, t + 1)
                for f in range(KC):
                    ins = pe.matmul(ps_zT[:, 0, KC * t + f:KC * t + f + 1], off1[:, f * P:(f + 1) * P], ones[:, 0:1],
                                    start=True, stop=True)
                ins.then_inc(w1_bias_mm, 1)

            with pe.Fori(0, (TILES - 2) // 2) as pair:
                i = 2 * pair
                attention_tile(i, 0)
                attention_tile(i + 1, 1)
            attention_tile(TILES - 2, 0, w1_bias=True)
            pe.wait_ge(w1_bias_ready, 1)
            attention_tile(TILES - 1, 1, project=False, y_rows=True)

            def hidden(n, c, j, s):
                if not (isinstance(n, int) and n < 2):
                    pe.wait_ge(h_ready, n - 1)
                cols = slice(c * P, (c + 1) * P)
                for k in range(KC):
                    ins = three(ps_unit[s][:, :], w1_hi[:, k, cols], w1_lo[:, k, cols], yT_hi[j][:, k, :],
                                yT_lo[j][:, k, :], k == 0, k == KC - 1)
                ins.then_inc(h_done, 1)

            def down(i, n, c, s, weights):
                pe.wait_ge(h_parts_ready, n + 1)
                if weights:
                    pe.wait_ge(w2_ready, c + 1)
                for t in range(SL):
                    if c == 0 and not first(i):
                        pe.wait_ge(out_ready, 4 * (i - 1) + t + 1)
                    rows = slice(t * P, (t + 1) * P)
                    ins = three(ps_acc[t], h_hi[:, s, rows], h_lo[:, s, rows], w2_hi[:, c, :], w2_lo[:, c, :],
                                c == 0, c == FC - 1)
                    if c == FC - 1:
                        ins.then_inc(acc_done, 1)
                if c < FC - 1:
                    ins.then_inc(mlp_done, 1)

            pe.wait_ge(zT_ready, LN2 + SL)
            pe.wait_ge(w1_ready, KC)
            hidden(0, 0, 0, 0)
            hidden(1, 1, 0, 1)

            def mlp_tile(i, j, ahead=True, weights=False):
                for c in range(FC):
                    if c + 2 < FC:
                        hidden(FC * i + c + 2, c + 2, j, c % 2)
                    elif ahead:
                        if c + 2 == FC:
                            pe.wait_ge(zT_ready, LN2 + 4 * (i + 2))
                        hidden(FC * i + c + 2, c + 2 - FC, 1 - j, c % 2)
                    down(i, FC * i + c, c, c % 2, weights)

            mlp_tile(0, 0, weights=True)
            with pe.Fori(0, (TILES - 2) // 2) as pair:
                i = 2 * pair + 1
                mlp_tile(i, 1)
                mlp_tile(i + 1, 0)
            mlp_tile(TILES - 1, 1, ahead=False)


_P = "L0_gnn_"
_INS = ["x", "adj"] + [_P + n for n in ("ln1_g", "ln1_b", "ln2_g", "ln2_b", "Wq", "bq", "Wk", "bk", "Wv", "bv",
                                        "Wo", "bo", "W1", "b1", "W2", "b2")]
_COLUMNS = [_P + n for n in ("ln1_g", "ln1_b", "ln2_g", "ln2_b", "bq", "bk", "bv", "b1")]


def kernel(**inputs):
    import numpy as _np
    import concourse.bacc as _bacc
    from concourse import mybir as _mybir
    from concourse.bass_utils import run_bass_kernel_spmd as _run

    nc = _bacc.Bacc("TRN2", target_bir_lowering=False, num_devices=1)
    arrays, args = {}, []
    for name in _INS:
        a = _np.asarray(inputs[name])
        if name in _COLUMNS:
            a = a.reshape(-1, 128).T
        a = _np.ascontiguousarray(a)
        arrays[f"in_{name}_dram"] = a
        args.append(nc.dram_tensor(f"in_{name}_dram", a.shape, _mybir.dt.from_np(a.dtype), kind="ExternalInput").ap())
    args.append(nc.dram_tensor("out_0_dram", inputs["x"].shape, _mybir.dt.float32, kind="ExternalOutput").ap())
    graph_layer(nc, *args)
    r = _run(nc, [arrays], core_ids=[0])
    return r.results[0]["out_0_dram"]
```

```python
import concourse.bass as bass
from concourse import mybir
from contextlib import ExitStack


def graph_layer(nc: bass.Bass, x, adj, ln1_g, ln1_b, ln2_g, ln2_b, Wq, bq, Wk, bk, Wv, bv, Wo, bo, W1, b1, W2, b2,
                out):
    fp32 = mybir.dt.float32
    f32r = mybir.dt.float32r
    u8 = mybir.dt.uint8
    ALU = mybir.AluOpType
    ACT = mybir.ActivationFunctionType
    AX = mybir.AxisListType

    GRAPHS, NODES, DIM = x.shape
    FF = W1.shape[1]
    HEADS, DH = 8, DIM // 8
    P = 128
    EPS = 1e-5
    NEG = -1.0e9
    KEEP = 3.0e38
    QSCALE = float(DH) ** -0.5

    KC = DIM // P
    HP = HEADS // 2
    FC = FF // P
    GS = P // NODES
    SL = 4
    TOK = SL * P
    GT = TOK // NODES
    TILES = GRAPHS * NODES // TOK
    UNITS = 3 * KC
    Q0, K0, V0 = 0, KC, 2 * KC
    assert UNITS == 3 * SL and TILES % 2 == 0 and TILES >= 6 and HP == KC and GS == 2

    x_v = x.rearrange("a s d -> (a s) d").rearrange("(n t p) d -> n t p d", t=SL, p=P)
    out_v = out.rearrange("a s d -> (a s) d").rearrange("(n t p) d -> n t p d", t=SL, p=P)
    x1_v = nc.dram_tensor("x1_rows", (GRAPHS * NODES, DIM), fp32, kind="Internal").ap()\
        .rearrange("(n t p) d -> n t p d", t=SL, p=P)
    adj_v = adj.rearrange("(n g) q k -> n q g k", g=GT)

    def chunked(w):
        return w.rearrange("(c p) n -> p c n", p=P)

    def row(v):
        return v.rearrange("(a n) -> a n", a=1).to_broadcast([P, v.shape[0]])

    ctx = ExitStack()
    with ctx:
        def keep(name, shape, dt=fp32):
            return ctx.enter_context(nc.sbuf_tensor(name, shape, dt))

        def sem(name):
            return ctx.enter_context(nc.semaphore(name))

        ident = keep("ident", [P, P])
        ones = keep("ones", [P, P])
        g1_col = keep("g1_col", [P, KC])
        b1n_col = keep("b1n_col", [P, KC])
        g2_col = keep("g2_col", [P, KC])
        b2n_col = keep("b2n_col", [P, KC])
        bq_col = keep("bq_col", [P, KC])
        bk_col = keep("bk_col", [P, KC])
        bv_col = keep("bv_col", [P, KC])
        bh_col = keep("bh_col", [P, FC])
        bo_row = keep("bo_row", [P, DIM])
        by_row = keep("by_row", [P, DIM])
        neg_half = keep("neg_half", [P, 1])
        eps = keep("eps", [P, 1])
        stats = keep("stats", [P, 2, 6])
        moments = keep("moments", [P, 2, 2])
        var_eps = keep("var_eps", [P, 2, 1])
        rstd = keep("rstd", [P, 2, 1])
        rowmax = keep("rowmax", [P, GS * HP])
        rowsum = keep("rowsum", [P, GS * HP])
        rowrec = keep("rowrec", [P, GS * HP])

        CH = 4 * DIM
        ARENA = 98 * CH
        arena = ctx.enter_context(nc.sbuf_tensor("arena", [P, ARENA // 4], fp32))
        base = nc.sbuf_base - ARENA

        def at(name, slot, shape, dt=fp32):
            return nc.alloc_sbuf_tensor_at(name, shape, dt, offset=base + int(slot * CH))

        wq_hi = at("wq_hi", 0, [P, KC, DIM], f32r)
        wq_lo = at("wq_lo", 4, [P, KC, DIM], f32r)
        wk_hi = at("wk_hi", 8, [P, KC, DIM], f32r)
        wk_lo = at("wk_lo", 12, [P, KC, DIM], f32r)
        wv_hi = at("wv_hi", 16, [P, KC, DIM], f32r)
        wv_lo = at("wv_lo", 20, [P, KC, DIM], f32r)
        zT_hi = [at(f"zT_hi{j}", 32 - 8 * j, [P, KC, TOK], f32r) for j in range(2)]
        zT_lo = [at(f"zT_lo{j}", 36 - 8 * j, [P, KC, TOK], f32r) for j in range(2)]
        wo_hi = at("wo_hi", 40, [P, KC, DIM], f32r)
        wo_lo = at("wo_lo", 44, [P, KC, DIM], f32r)
        qT = [at(f"qT{j}", 68 - 12 * j, [P, HP, TOK]) for j in range(2)]
        kT = [at(f"kT{j}", 72 - 12 * j, [P, HP, TOK]) for j in range(2)]
        v = [at(f"v{j}", 76 - 12 * j, [P, SL, DIM]) for j in range(2)]
        xs = at("xs", 80, [P, SL, DIM])
        z = at("z", 84, [P, 2, DIM])
        zT = at("zT", 85, [P, KC, P])
        xr = at("xr", 86, [P, SL, DIM])
        probs = at("probs", 90, [P, HP, GS, NODES])
        mask = at("mask", 91, [P, 2, GT, NODES])
        adj_b = at("adj_b", 93, [P, 2, GT, NODES], u8)
        probsT = at("probsT", 94, [P, HP, P])
        oT_hi = at("oT_hi", 95, [P, HP, P], f32r)
        oT_lo = at("oT_lo", 96, [P, HP, P], f32r)
        raw = [at("raw_q", 48, [P, KC, DIM]), at("raw_k", 52, [P, KC, DIM]), at("raw_v", 56, [P, KC, DIM]),
               at("raw_o", 60, [P, KC, DIM])]
        off = at("off", 64, [P, 4, DIM])
        prod = at("prod", 94, [P, KC, DIM])
        w1_hi = at("w1_hi", 0, [P, KC, FF], f32r)
        w1_lo = at("w1_lo", 16, [P, KC, FF], f32r)
        raw1 = [at("raw1_0", 48, [P, FF]), at("raw1_1", 52, [P, FF]), at("raw1_2", 32, [P, FF]),
                at("raw1_3", 36, [P, FF])]
        off1 = at("off1", 97, [P, DIM])
        w2_hi = at("w2_hi", 32, [P, FC, DIM], f32r)
        w2_lo = at("w2_lo", 48, [P, FC, DIM], f32r)
        yT_hi = [at(f"yT_hi{j}", 68 + 8 * j, [P, KC, TOK], f32r) for j in range(2)]
        yT_lo = [at(f"yT_lo{j}", 72 - 8 * j, [P, KC, TOK], f32r) for j in range(2)]
        ys = [at("ys0", 80, [P, SL, DIM]), at("ys1", 86, [P, SL, DIM])]
        h = at("h", 90, [P, 2, TOK])
        h_hi = at("h_hi", 95, [P, 2, TOK], f32r)
        h_lo = [at("h_lo0", 92, [P, TOK], f32r), at("h_lo1", 94, [P, TOK], f32r)]
        raw2 = [at("raw2_0", 93, [P, DIM]), at("raw2_1", 97, [P, DIM])]

        def bank(name, shape):
            return ctx.enter_context(nc.psum_tensor(name, shape, fp32))

        ps_unit = [bank(f"ps_unit{j}", [P, DIM]) for j in range(2)]
        ps_zT = bank("ps_zT", [P, KC, P])
        ps_s = bank("ps_s", [P, HP, GS, NODES])
        ps_pT = bank("ps_pT", [P, HP, P])
        ps_o = [bank(f"ps_o{g}", [P, DIM]) for g in range(GS)]
        ps_b1 = ps_o[0][:, HP * NODES:HP * NODES + FC]
        ps_x1 = bank("ps_x1", [P, DIM])
        ps_zT0 = [ps_zT, ps_x1[:, :].rearrange("p (c t) -> p c t", c=KC)]
        ps_acc = [ps_s[:, :, :, :].rearrange("p a b c -> p (a b c)"), ps_pT[:, :, :].rearrange("p a b -> p (a b)"),
                  ps_o[0][:, :], ps_o[1][:, :]]

        ident_set = sem("ident_set")
        cols_loaded = sem("cols_loaded")
        rows_loaded = sem("rows_loaded")
        raw_loaded = [sem(f"raw_loaded{m}") for m in range(4)]
        w_hi_ready = sem("w_hi_ready")
        w_ready = sem("w_ready")
        bias_mm = sem("bias_mm")
        bias_ready = sem("bias_ready")
        off_step = sem("off_step")
        prod_ready = sem("prod_ready")
        prod_halved = sem("prod_halved")
        off_q_ready = sem("off_q_ready")
        off_ready = sem("off_ready")
        bq_added = sem("bq_added")

        x_loaded = [sem(f"x_loaded{t}") for t in range(SL)]
        xr_loaded = [sem(f"xr_loaded{t}") for t in range(SL)]
        adj_loaded = [sem(f"adj_loaded{j}") for j in range(2)]
        mask_ready = sem("mask_ready")
        stats_ready = sem("stats_ready")
        moments_ready = sem("moments_ready")
        vareps_ready = sem("vareps_ready")
        rstd_ready = sem("rstd_ready")
        z_ready = sem("z_ready")
        zT_done = sem("zT_done")
        zT_hi_ready = sem("zT_hi_ready")
        zT_ready = sem("zT_ready")
        unit_done = sem("unit_done")
        unit_out = sem("unit_out")
        s_done = sem("s_done")
        masked = sem("masked")
        rowmax_ready = sem("rowmax_ready")
        shifted = sem("shifted")
        exp_ready = sem("exp_ready")
        rowsum_ready = sem("rowsum_ready")
        rowrec_ready = sem("rowrec_ready")
        probs_ready = sem("probs_ready")
        pT_done = sem("pT_done")
        pT_ready = sem("pT_ready")
        pv_done = sem("pv_done")
        oT_hi_ready = sem("oT_hi_ready")
        oT_ready = sem("oT_ready")
        o_done = sem("o_done")
        xr_ready = sem("xr_ready")
        x1_ready = sem("x1_ready")
        x1_stored = [sem(f"x1_stored{t}") for t in range(SL)]

        raw1_loaded = [sem(f"raw1_loaded{c}") for c in range(KC)]
        off1_step = sem("off1_step")
        off1_ready = sem("off1_ready")
        w1_scaled = sem("w1_scaled")
        w1_hi_ready = sem("w1_hi_ready")
        w1_ready = sem("w1_ready")
        w1_bias_mm = sem("w1_bias_mm")
        w1_bias_ready = sem("w1_bias_ready")
        raw2_loaded = [sem(f"raw2_loaded{j}") for j in range(2)]
        w2_hi_ready = sem("w2_hi_ready")
        w2_ready = sem("w2_ready")
        y_loaded = [[sem(f"y_loaded{j}_{t}") for t in range(SL)] for j in range(2)]
        yb_ready = sem("yb_ready")
        h_done = sem("h_done")
        h_ready = sem("h_ready")
        h_hi_ready = sem("h_hi_ready")
        h_parts_ready = sem("h_parts_ready")
        mlp_done = sem("mlp_done")
        acc_done = sem("acc_done")
        out_ready = sem("out_ready")
        out_stored = [sem(f"out_stored{t}") for t in range(SL)]

        block = ctx.enter_context(nc.Block())

        def first(i):
            return isinstance(i, int) and i == 0

        LN2 = TILES * SL

        @block.sync
        def _(sp):
            def load_x(i, t):
                if not (isinstance(i, int) and i < 1):
                    sp.wait_ge(z_ready, 4 * (i - 1) + t + 1)
                sp.dma_start(xs[:, t, :], x_v[i, t, :, :]).then_inc(x_loaded[t], 16)

            def load_xr(i, t):
                if not first(i):
                    sp.wait_ge(x1_stored[t], 16 * i)
                sp.dma_start(xr[:, t, :], x_v[i, t, :, :]).then_inc(xr_loaded[t], 16)

            def load_adj(i, j):
                for half in range(2):
                    sp.dma_start(adj_b[half * NODES:(half + 1) * NODES, j, :, :], adj_v[i, :, :, :])\
                      .then_inc(adj_loaded[j], 16)

            def store_x1(i, t):
                sp.wait_ge(x1_ready, 4 * i + t + 1)
                sp.dma_start(x1_v[i, t, :, :], xr[:, t, :]).then_inc(x1_stored[t], 16)

            for t in range(SL):
                load_x(0, t)
            for c, dst in ((ln1_g, g1_col), (ln1_b, b1n_col), (bq, bq_col), (bk, bk_col), (bv, bv_col)):
                sp.dma_start(dst[:, :], c).then_inc(cols_loaded, 16)
            for m, w in enumerate((Wq, Wk, Wv, Wo)):
                sp.dma_start(raw[m][:, :, :], chunked(w)).then_inc(raw_loaded[m], 16)
            for c, dst in ((ln2_g, g2_col), (ln2_b, b2n_col), (b1, bh_col)):
                sp.dma_start(dst[:, :], c).then_inc(rows_loaded, 16)
            for c, dst in ((bo, bo_row), (b2, by_row)):
                sp.dma_start(dst[:, :], row(c)).then_inc(rows_loaded, 16)
            load_adj(0, 0)
            load_adj(1, 1)
            for t in range(SL):
                load_xr(0, t)
            for t in range(SL):
                load_x(1, t)
            for t in range(SL):
                load_x(2, t)

            def attention_tile(i, j, next_x=True, phase_two=False):
                sp.wait_ge(mask_ready, i + 1)
                for t in range(SL):
                    if next_x:
                        load_x(i + 3, t)
                    store_x1(i, t)
                    if t:
                        load_xr(i + 1, t - 1)
                if phase_two:
                    sp.wait_ge(unit_done, UNITS * (i + 2))
                    for c in range(2, KC):
                        load_raw1(c)
                    for t in range(SL):
                        load_y(0, 0, t)
                load_xr(i + 1, SL - 1)
                if next_x or (isinstance(i, int) and i + 2 < TILES):
                    load_adj(i + 2, j)

            w1_v = W1.rearrange("(c p) n -> c p n", p=P)

            def load_raw1(c):
                sp.dma_start(raw1[c][:, :], w1_v[c, :, :]).then_inc(raw1_loaded[c], 16)

            def load_y(i, j, t):
                if isinstance(i, int) and i < 2:
                    sp.wait_ge(x1_stored[t], 16 * (i + 1))
                    if i == 0:
                        sp.wait_ge(z_ready, LN2)
                else:
                    sp.wait_ge(out_stored[t], 16 * (i - 1))
                sp.dma_start(ys[j][:, t, :], x1_v[i, t, :, :]).then_inc(y_loaded[j][t], 16)

            with sp.Fori(0, (TILES - 4) // 2) as pair:
                i = 2 * pair
                attention_tile(i, 0)
                attention_tile(i + 1, 1)
            attention_tile(TILES - 4, 0)
            sp.wait_ge(w_ready, 4 * KC)
            sp.wait_ge(bias_mm, 4)
            for c in range(2):
                load_raw1(c)
            attention_tile(TILES - 3, 1, next_x=False, phase_two=True)
            attention_tile(TILES - 2, 0, next_x=False)
            w2_v = W2.rearrange("(c p) n -> c p n", p=P)

            def load_raw2(c):
                if c >= 2:
                    sp.wait_ge(w2_ready, c - 1)
                sp.dma_start(raw2[c % 2][:, :], w2_v[c, :, :]).then_inc(raw2_loaded[c % 2], 16)

            sp.wait_ge(mask_ready, TILES)
            sp.wait_ge(w1_bias_mm, 4)
            for c in range(2):
                load_raw2(c)
            for t in range(SL):
                store_x1(TILES - 1, t)
            for t in range(SL):
                sp.wait_ge(x1_stored[t], 16 * TILES)
            for t in range(SL):
                load_y(1, 1, t)
            for c in range(2, FC):
                load_raw2(c)

            def store_out(i, j, t):
                sp.wait_ge(out_ready, 4 * i + t + 1)
                sp.dma_start(out_v[i, t, :, :], ys[j][:, t, :]).then_inc(out_stored[t], 16)

            def mlp_tile(i, j, more=True):
                for t in range(SL):
                    store_out(i, j, t)
                if more:
                    for t in range(SL):
                        load_y(i + 2, j, t)

            with sp.Fori(0, (TILES - 2) // 2) as pair:
                i = 2 * pair
                mlp_tile(i, 0)
                mlp_tile(i + 1, 1)
            for i in range(TILES - 2, TILES):
                mlp_tile(i, i % 2, more=False)
            for t in range(SL):
                sp.wait_ge(out_stored[t], 16 * TILES)

        @block.gpsimd
        def _(pool):
            pool.memset(ident[:, :], 0.0).then_inc(ident_set, 1)
            pool.memset(neg_half[:, :], -0.5).then_inc(ident_set, 1)
            pool.memset(eps[:, :], EPS).then_inc(ident_set, 1)
            pool.memset(ones[:, :], 1.0).then_inc(ident_set, 1)
            pool.wait_ge(ident_set, 4)
            pool.affine_select(out=ident[:, :], in_=ident[:, :], compare_op=ALU.not_equal, fill=1.0, base=0,
                               pattern=[[-1, P]], channel_multiplier=1).then_inc(ident_set, 1)

            def add_chunks(m):
                pool.wait_ge(prod_ready, KC * m)
                pool.tensor_tensor(prod[:, 0:2, :], prod[:, 0:2, :], prod[:, 2:4, :], ALU.add).then_inc(prod_halved, 1)
                pool.wait_ge(prod_halved, m)
                pool.tensor_tensor(off[:, m, :], prod[:, 0, :], prod[:, 1, :], ALU.add).then_inc(off_ready, 1)

            def norm_power(m, slot):
                pool.wait_ge(moments_ready, m + 1)
                pool.tensor_tensor(var_eps[:, slot, :], moments[:, slot, 1:2], eps[:, :], ALU.add)\
                    .then_inc(vareps_ready, 1)
                pool.wait_ge(vareps_ready, m + 1)
                pool.tensor_tensor(rstd[:, slot, :], var_eps[:, slot, :], neg_half[:, :], ALU.pow)\
                    .then_inc(rstd_ready, 1)

            def add_bias(i, t):
                pool.wait_ge(xr_loaded[t], 16 * (i + 1))
                pool.tensor_tensor(xr[:, t, :], xr[:, t, :], bo_row[:, :], ALU.add).then_inc(xr_ready, 1)

            for m in range(SL):
                norm_power(m, m % 2)
            add_chunks(1)
            norm_power(SL, 0)
            norm_power(SL + 1, 1)
            add_chunks(2)
            norm_power(SL + 2, 0)
            norm_power(SL + 3, 1)
            add_chunks(3)
            norm_power(2 * SL, 0)
            pool.wait_ge(bias_ready, 4)

            def attention_tile(i, norms=SL):
                for t in range(SL):
                    if t < norms:
                        norm_power(4 * (i + 2) + t + 1, (t + 1) % 2)
                    add_bias(i, t)

            with pool.Fori(0, (TILES - 4) // 2) as pair:
                i = 2 * pair
                attention_tile(i)
                attention_tile(i + 1)
            attention_tile(TILES - 4)
            attention_tile(TILES - 3, norms=SL - 1)
            attention_tile(TILES - 2, norms=0)

            def norm_rows(m, i, j, t):
                norm_power(LN2 + m, t % 2)
                pool.wait_ge(z_ready, LN2 + m + 1)
                pool.tensor_tensor(ys[j][:, t, :], ys[j][:, t, :], by_row[:, :], ALU.add).then_inc(yb_ready, 1)

            def cut_w1(c):
                pool.wait_ge(w1_hi_ready, c + 1)
                pool.tensor_tensor(w1_lo[:, c, :], raw1[c][:, :], w1_hi[:, c, :].bitcast(fp32), ALU.subtract)\
                    .then_inc(w1_ready, 1)

            pool.wait_ge(rows_loaded, 16 * 5)
            norm_rows(0, 0, 0, 0)
            add_bias(TILES - 1, 0)
            norm_rows(1, 0, 0, 1)
            for t in range(1, SL):
                add_bias(TILES - 1, t)
            for t in range(2, SL):
                norm_rows(t, 0, 0, t)
                cut_w1(t)
            for t in range(SL):
                norm_rows(4 + t, 1, 1, t)
            with pool.Fori(1, TILES // 2) as pair:
                i = 2 * pair
                for j in range(2):
                    for t in range(SL):
                        norm_rows(4 * (i + j) + t, i + j, j, t)

        @block.scalar
        def _(act):
            def cut_hi(w_hi, m, c, g):
                act.activation(w_hi[:, c, :], raw[m][:, c, :], ACT.Copy, scale=g).then_inc(w_hi_ready, 1)

            def out_zT(m, src, hi, t):
                act.wait_ge(zT_done, m + 1)
                act.activation(hi[:, :, t * P:(t + 1) * P], src[:, :, :], ACT.Copy).then_inc(zT_hi_ready, 1)

            def out_unit(i, j, u):
                act.wait_ge(unit_done, UNITS * i + u + 1)
                ps = ps_unit[u % 2]
                if u < K0:
                    ins = act.activation(qT[j][:, u, :], ps[:, :], ACT.Identity, bias=bq_col[:, u:u + 1],
                                         scale=QSCALE)
                elif u < V0:
                    c = u - K0
                    ins = act.activation(kT[j][:, c, :], ps[:, :], ACT.Identity, bias=bk_col[:, c:c + 1])
                else:
                    ins = act.activation(v[j][:, u - V0, :], ps[:, :], ACT.Copy)
                ins.then_inc(unit_out, 1)

            def out_pT(n):
                act.wait_ge(pT_done, n + 1)
                act.activation(probsT[:, :, :], ps_pT[:, :, :], ACT.Copy).then_inc(pT_ready, 1)

            def out_o(n):
                act.wait_ge(pv_done, n + 1)
                for g in range(GS):
                    act.activation(oT_hi[:, :, g * NODES:(g + 1) * NODES],
                                   ps_o[g][:, 0:HP * NODES].rearrange("p (h q) -> p h q", q=NODES), ACT.Copy)\
                       .then_inc(oT_hi_ready, 1)

            def exps(n):
                act.wait_ge(shifted, n + 1)
                act.activation(probs[:, :, :, :], probs[:, :, :, :], ACT.Exp).then_inc(exp_ready, 1)

            def cut(k):
                m, c = k // KC, k % KC
                if c == 0:
                    act.wait_ge(raw_loaded[m], 16)
                cut_hi((wq_hi, wk_hi, wv_hi, wo_hi)[m], m, c, g1_col[:, c:c + 1] if m < 3 else 1.0)

            def weigh(m):
                if m > 1:
                    act.wait_ge(off_ready, m - 1)
                for c in range(KC):
                    act.activation(prod[:, c, :], raw[m][:, c, :], ACT.Copy,
                                   scale=(b1n_col if m < 3 else bv_col)[:, c:c + 1]).then_inc(prod_ready, 1)

            for t in range(SL):
                out_zT(t, ps_zT0[t % 2], zT_hi[0], t)
                if t == 2:
                    act.wait_ge(cols_loaded, 16 * 5)
                    cut(0)
            for k in range(1, 2 * KC):
                cut(k)
            weigh(1)
            for u in range(UNITS):
                if u == 0 or u == K0:
                    act.wait_ge(bias_ready, 1 + u // KC)
                out_unit(0, 0, u)
                if 7 <= u < 7 + SL:
                    out_zT(u - 7 + SL, ps_zT, zT_hi[1], u - 7)
                if u < 4:
                    cut(2 * KC + u)
                if u == 2:
                    weigh(2)
                if 4 <= u < 6:
                    cut(2 * u + 4)
                    cut(2 * u + 5)
                if u == 10:
                    exps(0)
                if u == 6:
                    act.wait_ge(bias_ready, 3)
                    weigh(3)
            act.wait_ge(bias_ready, 4)

            def attention_tile(i, j, project=True, norm=True, weights=False):
                for t in range(SL):
                    n = 4 * i + t
                    out_pT(n)
                    if project:
                        out_unit(i + 1, 1 - j, 3 * t)
                    out_o(n)
                    if project or t < SL - 1:
                        exps(n + 1)
                    if project:
                        out_unit(i + 1, 1 - j, 3 * t + 1)
                    if norm:
                        out_zT(n + 2 * SL, zT, zT_hi[j], t)
                    if project:
                        out_unit(i + 1, 1 - j, 3 * t + 2)
                    if weights and t == 2:
                        act.wait_ge(unit_done, UNITS * (i + 1) + K0)
                        cut_w1(0)
                    if weights and t == 3:
                        cut_w1(1)
                        act.wait_ge(unit_done, UNITS * (i + 1) + V0)

            def cut_w1(c):
                act.wait_ge(raw1_loaded[c], 16)
                act.activation(w1_hi[:, c, :], raw1[c][:, :], ACT.Copy, scale=g2_col[:, c:c + 1])\
                   .then_inc(w1_hi_ready, 1)

            with act.Fori(0, (TILES - 2) // 2) as pair:
                i = 2 * pair
                attention_tile(i, 0)
                attention_tile(i + 1, 1)

            def scale_w1(c):
                act.activation(raw1[c][:, :], raw1[c][:, :], ACT.Copy, scale=g2_col[:, c:c + 1])\
                   .then_inc(w1_scaled, 1)

            def cut_scaled_w1(c):
                act.wait_ge(w1_scaled, c - 1)
                act.activation(w1_hi[:, c, :], raw1[c][:, :], ACT.Copy).then_inc(w1_hi_ready, 1)

            act.wait_ge(rows_loaded, 16 * 5)
            attention_tile(TILES - 2, 0, norm=False, weights=True)
            act.wait_ge(s_done, SL * (TILES - 1))
            out_zT(LN2, ps_zT, yT_hi[0], 0)
            for t in range(SL):
                n = 4 * (TILES - 1) + t
                out_pT(n)
                out_o(n)
                if t < SL - 1:
                    exps(n + 1)
                if t == 0:
                    act.wait_ge(off1_ready, 4)
                    scale_w1(2)
                    cut_scaled_w1(2)
                if t == 1:
                    scale_w1(3)
                    cut_scaled_w1(3)
                if t < SL - 1:
                    out_zT(LN2 + t + 1, ps_zT, yT_hi[0], t + 1)

            def cut_w2(c):
                act.wait_ge(raw2_loaded[c % 2], 16 * (c // 2 + 1))
                act.activation(w2_hi[:, c, :], raw2[c % 2][:, :], ACT.Copy).then_inc(w2_hi_ready, 1)

            def gelu(n, c, s):
                act.wait_ge(h_done, n + 1)
                if not (isinstance(n, int) and n < 2):
                    act.wait_ge(h_parts_ready, n - 1)
                act.activation(h[:, s, :], ps_unit[s][:, :], ACT.Gelu, bias=bh_col[:, c:c + 1]).then_inc(h_ready, 1)

            act.wait_ge(w1_ready, KC)
            cut_w2(0)
            act.wait_ge(w1_bias_ready, 1)
            gelu(0, 0, 0)
            cut_w2(1)
            gelu(1, 1, 1)

            def mlp_tile(i, j, ahead=True, weights=False):
                for c in range(FC):
                    if weights and c + 2 < FC:
                        cut_w2(c + 2)
                    if ahead or c + 2 < FC:
                        gelu(FC * i + c + 2, (c + 2) % FC, c % 2)
                    if ahead and c % 3 == 0 and 0 < c <= 3 * SL:
                        out_zT(LN2 + 4 * (i + 1) + c // 3 - 1, zT, yT_hi[1 - j], c // 3 - 1)

            mlp_tile(0, 0, weights=True)
            with act.Fori(0, (TILES - 2) // 2) as pair:
                i = 2 * pair + 1
                mlp_tile(i, 1)
                mlp_tile(i + 1, 0)
            mlp_tile(TILES - 1, 1, ahead=False)

        @block.vector
        def _(dve):
            def cut_lo(w_hi, w_lo, m, c, g, n):
                dve.wait_ge(w_hi_ready, n + 1)
                dve.scalar_tensor_tensor(out=w_lo[:, c, :], in0=raw[m][:, c, :], scalar=g,
                                         in1=w_hi[:, c, :].bitcast(fp32), op0=ALU.mult, op1=ALU.subtract)\
                   .then_inc(w_ready, 1)

            def row_stats(m, s, rows, behind=None):
                dve.bn_stats(stats[:, s, :], rows).then_inc(stats_ready, 1)
                dve.wait_ge(stats_ready, m + 1)
                if behind is not None:
                    behind()
                dve.bn_aggr(moments[:, s, :], stats[:, s, :]).then_inc(moments_ready, 1)

            def stats_x(i, t, behind=None):
                dve.wait_ge(x_loaded[t], 16 * (i + 1))
                row_stats(4 * i + t, t % 2, xs[:, t, :], behind)

            def normalise(m, s, rows, alternate=False):
                dve.wait_ge(rstd_ready, m + 1)
                if not (isinstance(m, int) and m < 2):
                    dve.wait_ge(zT_done, m - 1 if alternate else m)
                dve.tensor_scalar(z[:, s if alternate else 0, :], rows, moments[:, s, 0:1], rstd[:, s, 0:1],
                                  ALU.subtract, ALU.mult).then_inc(z_ready, 1)

            def turn(m):
                dve.wait_ge(z_ready, m + 1)
                rows = z[:, 0, :].rearrange("p (c f) -> p c f", f=P)
                for a in range(0, P, 32):
                    for b in range(0, P, 32):
                        ins = dve.transpose(zT[b:b + 32, :, a:a + 32], rows[a:a + 32, :, b:b + 32])
                ins.then_inc(zT_done, 1)

            def lo_zT(m, src, hi, lo, t):
                dve.wait_ge(zT_hi_ready, m + 1)
                cols = slice(t * P, (t + 1) * P)
                dve.tensor_tensor(lo[:, :, cols], src[:, :, :], hi[:, :, cols].bitcast(fp32), ALU.subtract)\
                   .then_inc(zT_ready, 1)

            def make_mask(i, j):
                if isinstance(i, int):
                    dve.wait_ge(adj_loaded[j], 32 * (i // 2 + 1))
                else:
                    dve.wait_ge(adj_loaded[j], 16 * (i - j) + 32)
                dve.tensor_scalar(mask[:, j, :, :], adj_b[:, j, :, :], KEEP, NEG, ALU.mult, ALU.add)\
                   .then_inc(mask_ready, 1)

            def softmax_front(n, i, j, t):
                dve.wait_ge(s_done, n + 1)
                dve.wait_ge(mask_ready, i + 1)
                m = mask[:, j, GS * t:GS * (t + 1), :].rearrange("p (a g) k -> p a g k", a=1)\
                    .to_broadcast([P, HP, GS, NODES])
                dve.tensor_tensor(probs[:, :, :, :], ps_s[:, :, :, :], m, ALU.min).then_inc(masked, 1)
                dve.wait_ge(masked, n + 1)
                p3 = probs[:, :, :, :].rearrange("p h g k -> p (h g) k")
                dve.tensor_reduce(rowmax[:, :], p3, AX.X, ALU.max).then_inc(rowmax_ready, 1)
                dve.wait_ge(rowmax_ready, n + 1)
                dve.tensor_tensor(p3, p3, spread(rowmax), ALU.subtract).then_inc(shifted, 1)

            def spread(rows):
                return rows[:, :].rearrange("p (h a) -> p h a", a=1).to_broadcast([P, GS * HP, NODES])

            def softmax_back(n):
                dve.wait_ge(exp_ready, n + 1)
                p3 = probs[:, :, :, :].rearrange("p h g k -> p (h g) k")
                dve.tensor_reduce(rowsum[:, :], p3, AX.X, ALU.add).then_inc(rowsum_ready, 1)
                dve.wait_ge(rowsum_ready, n + 1)
                dve.reciprocal(rowrec[:, :], rowsum[:, :]).then_inc(rowrec_ready, 1)
                dve.wait_ge(rowrec_ready, n + 1)
                dve.tensor_tensor(p3, p3, spread(rowrec), ALU.mult).then_inc(probs_ready, 1)

            def lo_o(n):
                for g in range(GS):
                    dve.wait_ge(oT_hi_ready, 2 * n + g + 1)
                    cols = slice(g * NODES, (g + 1) * NODES)
                    ins = dve.tensor_tensor(oT_lo[:, :, cols],
                                            ps_o[g][:, 0:HP * NODES].rearrange("p (h q) -> p h q", q=NODES),
                                            oT_hi[:, :, cols].bitcast(fp32), ALU.subtract)
                ins.then_inc(oT_ready, 1)

            def residual(n, t):
                dve.wait_ge(o_done, n + 1)
                dve.wait_ge(xr_ready, n + 1)
                dve.tensor_tensor(xr[:, t, :], ps_x1[:, :], xr[:, t, :], ALU.add).then_inc(x1_ready, 1)

            def cut(k):
                m, c = k // KC, k % KC
                hi, lo = ((wq_hi, wq_lo), (wk_hi, wk_lo), (wv_hi, wv_lo), (wo_hi, wo_lo))[m]
                if c == 0:
                    dve.wait_ge(raw_loaded[m], 16)
                cut_lo(hi, lo, m, c, g1_col[:, c:c + 1] if m < 3 else 1.0, k)

            def weigh(acc, chunks, col, step, steps, ready):
                dve.tensor_scalar(acc, chunks[0], col[:, 0:1], None, ALU.mult).then_inc(step, 1)
                for c in range(1, KC):
                    dve.wait_ge(step, steps + c)
                    dve.scalar_tensor_tensor(out=acc, in0=chunks[c], scalar=col[:, c:c + 1], in1=acc, op0=ALU.mult,
                                             op1=ALU.add).then_inc(ready if c == KC - 1 else step, 1)

            def add_bias(m, col, ps):
                dve.wait_ge(bias_mm, m + 1)
                return dve.tensor_tensor(col[:, :], ps, col[:, :], ALU.add)

            stats_x(0, 0)
            stats_x(0, 1)
            for t in range(SL):
                normalise(t, t % 2, xs[:, t, :], alternate=True)
                if t + 2 < SL:
                    stats_x(0, t + 2)
                if t:
                    lo_zT(t - 1, ps_zT0[(t - 1) % 2], zT_hi[0], zT_lo[0], t - 1)
            dve.wait_ge(cols_loaded, 16 * 5)
            cut(0)
            lo_zT(SL - 1, ps_zT0[(SL - 1) % 2], zT_hi[0], zT_lo[0], SL - 1)
            for k in range(1, KC):
                cut(k)
            weigh(off[:, 0, :], [raw[0][:, c, :] for c in range(KC)], b1n_col, off_step, 0, off_q_ready)
            for k in range(KC, 2 * KC):
                cut(k)
            add_bias(0, bq_col, ps_s[:, 0, 0, 0:KC]).then_inc(bq_added, 1)
            dve.wait_ge(bq_added, 1)
            dve.tensor_scalar(bq_col[:, :], bq_col[:, :], QSCALE, None, ALU.mult).then_inc(bias_ready, 1)
            add_bias(1, bk_col, ps_pT[:, 0, 0:KC]).then_inc(bias_ready, 1)
            stats_x(1, 0)
            stats_x(1, 1)
            for k in range(2 * KC, 3 * KC):
                cut(k)
            for t in range(SL):
                if t == 3:
                    make_mask(0, 0)
                    softmax_front(0, 0, 0, 0)
                normalise(SL + t, t % 2, xs[:, t, :], alternate=True)
                if t + 2 < SL:
                    stats_x(1, t + 2)
                if t == 1:
                    add_bias(2, bv_col, ps_o[0][:, 0:KC]).then_inc(bias_ready, 1)
                    for k in range(3 * KC, 4 * KC):
                        cut(k)
                if t:
                    lo_zT(SL + t - 1, ps_zT, zT_hi[1], zT_lo[1], t - 1)
            softmax_back(0)
            stats_x(2, 0)
            lo_zT(2 * SL - 1, ps_zT, zT_hi[1], zT_lo[1], SL - 1)
            dve.wait_ge(rows_loaded, 16 * 5)
            add_bias(3, bo_row, ps_x1[:, :]).then_inc(bias_ready, 1)

            def stats_y(i, j, t, behind=None):
                if isinstance(i, int):
                    dve.wait_ge(y_loaded[j][t], 16 * (i // 2 + 1))
                else:
                    dve.wait_ge(y_loaded[j][t], 8 * (i - j) + 16)
                row_stats(LN2 + 4 * i + t, t % 2, ys[j][:, t, :], behind)

            def weigh_w1(t):
                for c in range(KC):
                    dve.wait_ge(raw1_loaded[c], 16)
                if t:
                    dve.wait_ge(w1_bias_mm, t)
                weigh(off1[:, :], [raw1[c][:, t * DIM:(t + 1) * DIM] for c in range(KC)], b2n_col, off1_step,
                      (KC - 1) * t, off1_ready)

            def attention_tile(i, j, project=True, norm=True, more_rows=True, w1_bias=False):
                for t in range(SL):
                    n = 4 * i + t
                    if norm:
                        def rows_now():
                            normalise(n + 2 * SL, t % 2, xs[:, t, :])

                        if t < SL - 1:
                            stats_x(i + 2, t + 1, rows_now)
                        elif more_rows:
                            stats_x(i + 3, 0, rows_now)
                        else:
                            rows_now()
                        turn(n + 2 * SL)
                    if w1_bias and t == SL - 1:
                        stats_y(0, 0, 0)
                        normalise(LN2, 0, ys[0][:, 0, :], alternate=True)
                    if project or t < SL - 1:
                        if t < SL - 1:
                            softmax_front(n + 1, i, j, t + 1)
                        else:
                            make_mask(i + 1, 1 - j)
                            softmax_front(n + 1, i + 1, 1 - j, 0)
                    lo_o(n)
                    if project or t < SL - 1:
                        softmax_back(n + 1)
                    if w1_bias:
                        weigh_w1(t)
                    if norm:
                        lo_zT(n + 2 * SL, zT, zT_hi[j], zT_lo[j], t)
                    if w1_bias and t == SL - 1:
                        lo_zT(LN2, ps_zT, yT_hi[0], yT_lo[0], 0)
                    residual(n, t)

            with dve.Fori(0, (TILES - 4) // 2) as pair:
                i = 2 * pair
                attention_tile(i, 0)
                attention_tile(i + 1, 1)
            attention_tile(TILES - 4, 0)
            attention_tile(TILES - 3, 1, more_rows=False)
            dve.wait_ge(rows_loaded, 16 * 5)
            attention_tile(TILES - 2, 0, norm=False, w1_bias=True)

            def cut_w1(c):
                dve.wait_ge(w1_hi_ready, c + 1)
                dve.scalar_tensor_tensor(out=w1_lo[:, c, :], in0=raw1[c][:, :], scalar=g2_col[:, c:c + 1],
                                         in1=w1_hi[:, c, :].bitcast(fp32), op0=ALU.mult, op1=ALU.subtract)\
                   .then_inc(w1_ready, 1)

            last = TILES - 1
            dve.wait_ge(w1_bias_mm, 4)
            dve.tensor_tensor(bh_col[:, :], ps_b1[:, :], bh_col[:, :], ALU.add).then_inc(w1_bias_ready, 1)
            dve.wait_ge(unit_done, UNITS * TILES)
            for t in range(SL):
                n = 4 * last + t
                if t < SL - 1:
                    softmax_front(n + 1, last, last % 2, t + 1)
                    lo_o(n)
                    softmax_back(n + 1)
                    stats_y(0, 0, t + 1)
                    if t == 0:
                        cut_w1(0)
                    normalise(LN2 + t + 1, (t + 1) % 2, ys[0][:, t + 1, :], alternate=True)
                    lo_zT(LN2 + t + 1, ps_zT, yT_hi[0], yT_lo[0], t + 1)
                    residual(n, t)
                else:
                    cut_w1(1)
                    lo_o(n)
            dve.wait_ge(w1_ready, KC)

            def cut_w2(c):
                dve.wait_ge(w2_hi_ready, c + 1)
                dve.tensor_tensor(w2_lo[:, c, :], raw2[c % 2][:, :], w2_hi[:, c, :].bitcast(fp32), ALU.subtract)\
                   .then_inc(w2_ready, 1)

            def cut_h(i, c, s):
                n = FC * i + c
                dve.wait_ge(h_ready, n + 1)
                if c == 1 and not first(i):
                    dve.wait_ge(acc_done, SL * i)
                elif c >= 2 or not first(i):
                    dve.wait_ge(mlp_done, (FC - 1) * i + max(c - 1, 0))
                dve.tensor_copy(h_hi[:, s, :], h[:, s, :]).then_inc(h_hi_ready, 1)
                dve.wait_ge(h_hi_ready, n + 1)
                dve.tensor_tensor(h_lo[s][:, :], h[:, s, :], h_hi[:, s, :].bitcast(fp32), ALU.subtract)\
                   .then_inc(h_parts_ready, 1)

            def finish(i, j, t):
                dve.wait_ge(acc_done, 4 * i + t + 1)
                dve.wait_ge(yb_ready, 4 * i + t + 1)
                dve.tensor_tensor(ys[j][:, t, :], ps_acc[t], ys[j][:, t, :], ALU.add).then_inc(out_ready, 1)

            cut_w2(0)
            residual(LN2 - 1, SL - 1)
            cut_h(0, 0, 0)
            cut_w2(1)
            cut_h(0, 1, 1)

            def mlp_tile(i, j, ahead=True, weights=False, before=True):
                for c in range(FC):
                    if weights and c + 2 < FC:
                        cut_w2(c + 2)
                    if c == 0 and before:
                        for t in range(SL):
                            finish(i - 1, 1 - j, t)
                    t = (c - 2) // 3
                    if ahead and c % 3 == 1 and 0 <= t < SL:
                        lo_zT(LN2 + 4 * (i + 1) + t, zT, yT_hi[1 - j], yT_lo[1 - j], t)
                    turned = c // 3 - 1
                    if ahead and c % 3 == 0 and 0 <= turned < SL:
                        normalise(LN2 + 4 * (i + 1) + turned, turned % 2, ys[1 - j][:, turned, :])

                    def part():
                        if c + 2 < FC:
                            cut_h(i, c + 2, c % 2)
                        else:
                            cut_h(i + 1, c + 2 - FC, c % 2)

                    if ahead and c % 3 == 2 and t < SL:
                        stats_y(i + 1, 1 - j, t, part)
                    elif ahead or c + 2 < FC:
                        part()
                    if ahead and c % 3 == 0 and 0 <= turned < SL:
                        turn(LN2 + 4 * (i + 1) + turned)

            mlp_tile(0, 0, weights=True, before=False)
            with dve.Fori(0, (TILES - 2) // 2) as pair:
                i = 2 * pair + 1
                mlp_tile(i, 1)
                mlp_tile(i + 1, 0)
            mlp_tile(TILES - 1, 1, ahead=False)
            for t in range(SL):
                finish(TILES - 1, 1, t)

        @block.tensor
        def _(pe):
            def three(ps, lhs_hi, lhs_lo, rhs_hi, rhs_lo, start, stop):
                pe.matmul(ps, lhs_hi, rhs_lo, start=start, stop=False)
                pe.matmul(ps, lhs_lo, rhs_hi, start=False, stop=False)
                return pe.matmul(ps, lhs_hi, rhs_hi, start=False, stop=stop)

            def transpose_rows(m, s, dst, before):
                pe.wait_ge(z_ready, m + 1)
                if before > 0:
                    pe.wait_ge(zT_ready, before)
                for c in range(KC):
                    ins = pe.transpose(dst[:, c, :], z[:, s, c * P:(c + 1) * P], ident[:, :])
                ins.then_inc(zT_done, 1)

            def unit(i, j, u, behind=None, weights=False):
                if u == 0:
                    pe.wait_ge(zT_ready, 4 * (i + 1))
                if not (isinstance(i, int) and UNITS * i + u < 2):
                    pe.wait_ge(unit_out, UNITS * i + u - 1)
                ps = ps_unit[u % 2][:, :]
                for c in range(KC):
                    if c == KC - 1 and behind is not None:
                        behind()
                    if weights:
                        pe.wait_ge(w_ready, KC * (u // KC) + c + 1)
                    if u < V0:
                        hi, lo = (wq_hi, wq_lo) if u < K0 else (wk_hi, wk_lo)
                        cols = slice(u % KC * P, (u % KC + 1) * P)
                        ins = three(ps, hi[:, c, cols], lo[:, c, cols], zT_hi[j][:, c, :], zT_lo[j][:, c, :],
                                    c == 0, c == KC - 1)
                    else:
                        rows = slice((u - V0) * P, (u - V0 + 1) * P)
                        ins = three(ps, zT_hi[j][:, c, rows], zT_lo[j][:, c, rows], wv_hi[:, c, :], wv_lo[:, c, :],
                                    c == 0, c == KC - 1)
                ins.then_inc(unit_done, 1)

            def await_scores(n, i, t):
                if t == 0:
                    pe.wait_ge(unit_out, UNITS * i + V0)
                if not (isinstance(n, int) and n < 1):
                    pe.wait_ge(masked, n)

            def scores(n, j, t):
                for g in range(GS):
                    tokens = slice((GS * t + g) * NODES, (GS * t + g + 1) * NODES)
                    for hp in range(HP):
                        for e in range(2):
                            rows = slice(e * DH, (e + 1) * DH)
                            ins = pe.matmul(ps_s[rows, hp, g, :], qT[j][rows, hp, tokens], kT[j][rows, hp, tokens],
                                            start=True, stop=True)
                ins.then_inc(s_done, 1)

            def transpose_probs(n):
                pe.wait_ge(probs_ready, n + 1)
                for hp in range(HP):
                    ins = pe.transpose(ps_pT[:, hp, :], probs[:, hp, :, :].rearrange("p g k -> p (g k)"), ident[:, :])
                ins.then_inc(pT_done, 1)

            def await_attend(n, i, t):
                if t == 0:
                    pe.wait_ge(unit_out, UNITS * (i + 1))
                pe.wait_ge(pT_ready, n + 1)

            def attend(n, j, t):
                for d in range(2):
                    for hp in range(HP):
                        for g in range(GS):
                            e = (g + d) % 2
                            rows = slice(g * NODES, (g + 1) * NODES)
                            head = 2 * hp + e
                            ins = pe.matmul(ps_o[g][e * DH:(e + 1) * DH, hp * NODES:(hp + 1) * NODES],
                                            v[j][rows, t, head * DH:(head + 1) * DH],
                                            probsT[rows, hp, e * NODES:(e + 1) * NODES], start=True, stop=True)
                ins.then_inc(pv_done, 1)

            def project_out(n):
                pe.wait_ge(oT_ready, n + 1)
                if not (isinstance(n, int) and n < 1):
                    pe.wait_ge(x1_ready, n)
                for c in range(KC):
                    ins = three(ps_x1[:, :], oT_hi[:, c, :], oT_lo[:, c, :], wo_hi[:, c, :], wo_lo[:, c, :],
                                c == 0, c == KC - 1)
                ins.then_inc(o_done, 1)

            def bias_column(m, dst):
                if m == 0:
                    pe.wait_ge(off_q_ready, 1)
                else:
                    pe.wait_ge(off_ready, m)
                for o in range(KC):
                    ins = pe.matmul(dst[:, o:o + 1], off[:, m, o * P:(o + 1) * P], ones[:, 0:1], start=True,
                                    stop=True)
                ins.then_inc(bias_mm, 1)

            pe.wait_ge(ident_set, 5)
            for t in range(SL):
                transpose_rows(t, t % 2, ps_zT0[t % 2], t - 1)
            for u in range(UNITS):
                unit(0, 0, u, weights=u % KC == 0)
                if u == 0:
                    bias_column(0, ps_s[:, 0, 0, :])
                if u == 3:
                    bias_column(1, ps_pT[:, 0, :])
                if u == 6:
                    bias_column(2, ps_o[0])
                if 7 <= u < 7 + SL:
                    transpose_rows(SL + u - 7, (u - 7) % 2, ps_zT, SL + u - 7)
                if u == 8:
                    pe.wait_ge(bias_ready, 1)
                    await_scores(0, 0, 0)
                    scores(0, 0, 0)
                if u == UNITS - 1:
                    pe.wait_ge(off_ready, 3)
                    pe.matmul(ps_x1[:, :], ones[:, :], off[:, 3, :], start=True, stop=True).then_inc(bias_mm, 1)
            pe.wait_ge(bias_ready, 4)
            pe.wait_ge(w_ready, 4 * KC)

            def attention_tile(i, j, project=True, w1_bias=False, y_rows=False):
                for t in range(SL):
                    n = 4 * i + t

                    def awaits():
                        if t < SL - 1:
                            await_scores(n + 1, i, t + 1)
                        elif project:
                            await_scores(n + 1, i + 1, 0)
                        await_attend(n, i, t)

                    transpose_probs(n)
                    if project:
                        unit(i + 1, 1 - j, 3 * t, awaits)
                    elif t < SL - 1:
                        await_scores(n + 1, i, t + 1)
                    if t < SL - 1:
                        scores(n + 1, j, t + 1)
                    elif project:
                        scores(n + 1, 1 - j, 0)
                    if not project:
                        await_attend(n, i, t)
                        if t == 0:
                            pe.wait_ge(w1_bias_ready, 1)
                    attend(n, j, t)
                    if project:
                        unit(i + 1, 1 - j, 3 * t + 1)
                        unit(i + 1, 1 - j, 3 * t + 2)
                    if w1_bias and t == SL - 1:
                        transpose_rows(LN2, 0, ps_zT, LN2)
                    project_out(n)
                    if w1_bias:
                        bias_w1(t)
                    if y_rows and t < SL - 1:
                        transpose_rows(LN2 + t + 1, (t + 1) % 2, ps_zT, LN2 + t + 1)

            def bias_w1(t):
                pe.wait_ge(off1_ready, t + 1)
                for f in range(KC):
                    ins = pe.matmul(ps_b1[:, KC * t + f:KC * t + f + 1], off1[:, f * P:(f + 1) * P], ones[:, 0:1],
                                    start=True, stop=True)
                ins.then_inc(w1_bias_mm, 1)

            with pe.Fori(0, (TILES - 2) // 2) as pair:
                i = 2 * pair
                attention_tile(i, 0)
                attention_tile(i + 1, 1)
            attention_tile(TILES - 2, 0, w1_bias=True)
            attention_tile(TILES - 1, 1, project=False, y_rows=True)

            def hidden(n, c, j, s):
                if not (isinstance(n, int) and n < 2):
                    pe.wait_ge(h_ready, n - 1)
                cols = slice(c * P, (c + 1) * P)
                for k in range(KC):
                    ins = three(ps_unit[s][:, :], w1_hi[:, k, cols], w1_lo[:, k, cols], yT_hi[j][:, k, :],
                                yT_lo[j][:, k, :], k == 0, k == KC - 1)
                ins.then_inc(h_done, 1)

            def down(i, n, c, s, weights):
                pe.wait_ge(h_parts_ready, n + 1)
                if weights:
                    pe.wait_ge(w2_ready, c + 1)
                for t in range(SL):
                    if c == 0 and not first(i):
                        pe.wait_ge(out_ready, 4 * (i - 1) + t + 1)
                    rows = slice(t * P, (t + 1) * P)
                    ins = three(ps_acc[t], h_hi[:, s, rows], h_lo[s][:, rows], w2_hi[:, c, :], w2_lo[:, c, :],
                                c == 0, c == FC - 1)
                    if c == FC - 1:
                        ins.then_inc(acc_done, 1)
                if c < FC - 1:
                    ins.then_inc(mlp_done, 1)

            pe.wait_ge(zT_ready, LN2 + SL)
            pe.wait_ge(w1_ready, KC)
            hidden(0, 0, 0, 0)
            hidden(1, 1, 0, 1)

            def mlp_tile(i, j, ahead=True, weights=False):
                for c in range(FC):
                    if c + 2 < FC:
                        hidden(FC * i + c + 2, c + 2, j, c % 2)
                    elif ahead:
                        if c + 2 == FC:
                            pe.wait_ge(zT_ready, LN2 + 4 * (i + 2))
                        hidden(FC * i + c + 2, c + 2 - FC, 1 - j, c % 2)
                    down(i, FC * i + c, c, c % 2, weights)

            mlp_tile(0, 0, weights=True)
            with pe.Fori(0, (TILES - 2) // 2) as pair:
                i = 2 * pair + 1
                mlp_tile(i, 1)
                mlp_tile(i + 1, 0)
            mlp_tile(TILES - 1, 1, ahead=False)


_P = "L0_gnn_"
_INS = ["x", "adj"] + [_P + n for n in ("ln1_g", "ln1_b", "ln2_g", "ln2_b", "Wq", "bq", "Wk", "bk", "Wv", "bv",
                                        "Wo", "bo", "W1", "b1", "W2", "b2")]
_COLUMNS = [_P + n for n in ("ln1_g", "ln1_b", "ln2_g", "ln2_b", "bq", "bk", "bv", "b1")]


def kernel(**inputs):
    import numpy as _np
    import concourse.bacc as _bacc
    from concourse import mybir as _mybir
    from concourse.bass_utils import run_bass_kernel_spmd as _run

    nc = _bacc.Bacc("TRN2", target_bir_lowering=False, num_devices=1)
    arrays, args = {}, []
    for name in _INS:
        a = _np.asarray(inputs[name])
        if name in _COLUMNS:
            a = a.reshape(-1, 128).T
        a = _np.ascontiguousarray(a)
        arrays[f"in_{name}_dram"] = a
        args.append(nc.dram_tensor(f"in_{name}_dram", a.shape, _mybir.dt.from_np(a.dtype), kind="ExternalInput").ap())
    args.append(nc.dram_tensor("out_0_dram", inputs["x"].shape, _mybir.dt.float32, kind="ExternalOutput").ap())
    graph_layer(nc, *args)
    r = _run(nc, [arrays], core_ids=[0])
    return r.results[0]["out_0_dram"]
```
